# Optimizing a Trainium2 kernel written in Bass

```python
import numpy as np
import jax
import jax.numpy as jnp

def _softmax(x, axis=-1):
    return jax.nn.softmax(x, axis=axis)

def _gelu(x):
    return jax.nn.gelu(x, approximate=True)

def _silu(x):
    return jax.nn.silu(x)

def _sigmoid(x):
    return jax.nn.sigmoid(x)

def _layernorm(x, axis=-1, eps=1e-05):
    m = jnp.mean(x, axis=axis, keepdims=True)
    v = jnp.var(x, axis=axis, keepdims=True)
    return (x - m) / jnp.sqrt(v + eps)

def _scatter_add(tgt, idx, src, axis=0):
    return tgt.at[idx].add(src)

def _segment_sum(src, seg, n):
    return jax.ops.segment_sum(src, seg, n)
kernel_name = 'mk_seq_postln_d1_jaxref_r4_dbea7f'

def setup_inputs(seed: int=0):
    np.random.seed(seed)
    _w = jnp.asarray

    def _L0_attn_setup():
        import jax, jax.numpy as jnp
        import numpy as np
        HIDDEN = 1024
        NUM_HEADS = 32
        HEAD_DIM = HIDDEN // NUM_HEADS
        THRESH = 0.001
        key = jax.random.key(seed)
        ks = jax.random.split(key, 9)
        w_std = 0.02
        x = jax.random.normal(ks[0], (4, 1024, HIDDEN), dtype=jnp.float32)
        Wq = jax.random.normal(ks[1], (HIDDEN, HIDDEN), dtype=jnp.float32) * w_std
        bq = jax.random.normal(ks[2], (HIDDEN,), dtype=jnp.float32) * w_std
        Wk = jax.random.normal(ks[3], (HIDDEN, HIDDEN), dtype=jnp.float32) * w_std
        bk = jax.random.normal(ks[4], (HIDDEN,), dtype=jnp.float32) * w_std
        Wv = jax.random.normal(ks[5], (HIDDEN, HIDDEN), dtype=jnp.float32) * w_std
        bv = jax.random.normal(ks[6], (HIDDEN,), dtype=jnp.float32) * w_std
        Wo = jax.random.normal(ks[7], (HIDDEN, HIDDEN), dtype=jnp.float32) * w_std
        bo = jax.random.normal(ks[8], (HIDDEN,), dtype=jnp.float32) * w_std
        return {'x': x, 'Wq': Wq, 'bq': bq, 'Wk': Wk, 'bk': bk, 'Wv': Wv, 'bv': bv, 'Wo': Wo, 'bo': bo}
    _L0_attn_in = _L0_attn_setup()

    def _L0_ffn_setup():
        import jax, jax.numpy as jnp
        import numpy as np
        HIDDEN = 1024
        INTER = 2752

        def _ternary_quantize(w):
            scale = jnp.mean(jnp.abs(w))
            return jnp.clip(jnp.round(w / scale), -1.0, 1.0) * scale
        key = jax.random.key(seed)
        kx, kg, ku, kd = jax.random.split(key, 4)
        x = jax.random.normal(kx, (2, 512, HIDDEN), dtype=jnp.float32)
        w_gate = _ternary_quantize(jax.random.normal(kg, (INTER, HIDDEN), dtype=jnp.float32) * 0.02)
        w_up = _ternary_quantize(jax.random.normal(ku, (INTER, HIDDEN), dtype=jnp.float32) * 0.02)
        w_down = _ternary_quantize(jax.random.normal(kd, (HIDDEN, INTER), dtype=jnp.float32) * 0.02)
        return {'x': x, 'w_gate': w_gate, 'w_up': w_up, 'w_down': w_down}
    _L0_ffn_in = _L0_ffn_setup()
    _d = {'L0_attn_x': _L0_attn_in['x'], 'L0_attn_Wq': _L0_attn_in['Wq'], 'L0_attn_bq': _L0_attn_in['bq'], 'L0_attn_Wk': _L0_attn_in['Wk'], 'L0_attn_bk': _L0_attn_in['bk'], 'L0_attn_Wv': _L0_attn_in['Wv'], 'L0_attn_bv': _L0_attn_in['bv'], 'L0_attn_Wo': _L0_attn_in['Wo'], 'L0_attn_bo': _L0_attn_in['bo'], 'L0_ffn_w_gate': _L0_ffn_in['w_gate'], 'L0_ffn_w_up': _L0_ffn_in['w_up'], 'L0_ffn_w_down': _L0_ffn_in['w_down']}
    _x0 = _d['L0_attn_x']
    _d['L0_attn_x'] = jax.random.normal(jax.random.fold_in(jax.random.key(seed), 1), (2, 1024, 1024), dtype=_x0.dtype)
    del _x0
    return _d

def reference(L0_attn_x, L0_attn_Wq, L0_attn_bq, L0_attn_Wk, L0_attn_bk, L0_attn_Wv, L0_attn_bv, L0_attn_Wo, L0_attn_bo, L0_ffn_w_gate, L0_ffn_w_up, L0_ffn_w_down):

    def _L0_attn_ref(x, Wq, bq, Wk, bk, Wv, bv, Wo, bo):
        import jax, jax.numpy as jnp
        import numpy as np
        HIDDEN = 1024
        NUM_HEADS = 32
        HEAD_DIM = HIDDEN // NUM_HEADS
        THRESH = 0.001
        B, S, Hd = x.shape
        H, D = (NUM_HEADS, HEAD_DIM)
        q = (x @ Wq.T + bq).reshape(B, S, H, D)
        k = (x @ Wk.T + bk).reshape(B, S, H, D)
        v = (x @ Wv.T + bv).reshape(B, S, H, D)
        inv_sqrt_d = np.float32(1.0 / np.sqrt(D))
        scores = jnp.einsum('bshd,bsgd->bshg', q, k) * inv_sqrt_d
        scores = jnp.where(scores > THRESH, scores, -jnp.inf)
        attn = jax.nn.softmax(scores, axis=-1)
        out = jnp.einsum('bshg,bsgd->bshd', attn, v).reshape(B, S, Hd)
        return out @ Wo.T + bo

    def _L0_ffn_ref(x, w_gate, w_up, w_down):
        import jax, jax.numpy as jnp
        import numpy as np
        HIDDEN = 1024
        INTER = 2752

        def _ternary_quantize(w):
            scale = jnp.mean(jnp.abs(w))
            return jnp.clip(jnp.round(w / scale), -1.0, 1.0) * scale
        xf = x.astype(jnp.float32) / 128.0
        gate = jnp.einsum('bsh,ih->bsi', xf, w_gate)
        up = jnp.einsum('bsh,ih->bsi', xf, w_up)
        inter = jax.nn.silu(gate) * up
        inter_q = jnp.trunc(jnp.clip(inter * 128.0, -128.0, 127.0)).astype(jnp.int8)
        down = jnp.einsum('bsi,hi->bsh', inter_q.astype(jnp.float32), w_down)
        out = jnp.trunc(jnp.clip(down * 128.0, -128.0, 127.0)).astype(jnp.int8)
        return out
    x = L0_attn_x
    x = _layernorm(x + _L0_attn_ref(x, L0_attn_Wq, L0_attn_bq, L0_attn_Wk, L0_attn_bk, L0_attn_Wv, L0_attn_bv, L0_attn_Wo, L0_attn_bo), axis=-1)
    x = _layernorm(x + _L0_ffn_ref(x, L0_ffn_w_gate, L0_ffn_w_up, L0_ffn_w_down), axis=-1)
    return x

_drawn_inputs = setup_inputs


def setup_inputs(seed=0):
    import zlib

    import numpy as np

    out = dict(_drawn_inputs(seed))
    spreads = {}
    factors = {'L0_attn_bq': 5.955, 'L0_attn_bk': 6.077, 'L0_attn_bv': 8.0, 'L0_attn_bo': 3.007}
    for name, (base, spread) in spreads.items():
        noise = np.random.default_rng([zlib.crc32(name.encode()), seed]).standard_normal(out[name].shape)
        drawn = base * np.exp(spread * noise) if base else spread * noise
        out[name] = jnp.asarray(drawn.astype(out[name].dtype))
    for name, factor in factors.items():
        out[name] = (out[name] * factor).astype(out[name].dtype)
    return out
```

```python
from contextlib import ExitStack

import numpy as np

import concourse.bass as bass
from concourse import mybir
from concourse.alu_op_type import AluOpType as ALU

F32 = mybir.dt.float32
F32R = mybir.dt.float32r
BF16 = mybir.dt.bfloat16
ACT = mybir.ActivationFunctionType
AX = mybir.AxisListType

P = 128
TOKENS = 2048
HID = 1024
KT = HID // P
HEADS = 32
HD = HID // HEADS
INTER = 2752
EPS = 1e-5

CHUNK = 512
CHUNKS = TOKENS // CHUNK
SUB = CHUNK // 4
SLOTS = 3
QKV_TILES = 3 * HID // P
ITERS = QKV_TILES // SLOTS
QUADS = 16
BATCHES = SUB // QUADS
HALF = SUB // 2
LAG = ITERS + 2
QKV_ITERS = CHUNKS * ITERS
ATT_BATCHES = CHUNKS * BATCHES
LOADS_PER_HALF = 3 * 4 * 16
SOFTMAX_STEPS = 7

FCH = 1024
FCHUNKS = TOKENS // FCH
FT = FCH // P
GTILES = INTER // P
REST = INTER - GTILES * P
ICH = GTILES + 1
ROUND = 1.5 * 2.0**23
OUT_TILES = TOKENS // P


def score_scale():
    return np.float32(1.0 / np.sqrt(HD))


def raw_threshold():
    scale, limit = score_scale(), np.float32(0.001)
    s = np.float32(limit / scale)
    while np.float32(s * scale) > limit:
        s = np.nextafter(s, np.float32(0), dtype=np.float32)
    while np.float32(np.nextafter(s, np.float32(1), dtype=np.float32) * scale) <= limit:
        s = np.nextafter(s, np.float32(1), dtype=np.float32)
    return float(s)


def loop(eng, first, count, body):
    if count == 1:
        body(first)
    else:
        with eng.Fori(first, first + count) as i:
            body(i)


def at(eng, value):
    return value if isinstance(value, int) else eng.snap(value)


def attention_stage(nc, x_t, w_qkv, b_qkv, qkv_dram, o_dram):
    scale, threshold = float(score_scale()), raw_threshold()
    with ExitStack() as ctx:
        def sb(name, shape, dt=F32):
            return ctx.enter_context(nc.sbuf_tensor(name, shape, dt))

        def sem(name):
            return ctx.enter_context(nc.semaphore(name))

        bias = sb("bias", [P, QKV_TILES])
        x_raw = sb("x_raw", [P, KT, CHUNK])
        x_hi = sb("x_hi", [P, KT, CHUNK], F32R)
        x_lo = sb("x_lo", [P, KT, CHUNK], F32R)
        w_raw = [sb(f"w_raw{s}", [P, KT, P]) for s in range(SLOTS)]
        w_hi = [sb(f"w_hi{s}", [P, KT, P], F32R) for s in range(SLOTS)]
        w_lo = [sb(f"w_lo{s}", [P, KT, P], F32R) for s in range(SLOTS)]
        stage = [sb(f"stage{s}", [P, CHUNK]) for s in range(SLOTS)]
        q_in = sb("q_in", [P, HEADS, SUB])
        k_in = sb("k_in", [P, HEADS, SUB])
        v_in = sb("v_in", [P, HEADS, SUB])
        q_diag = sb("q_diag", [P, QUADS, 4, HEADS])
        v_diag = sb("v_diag", [P, QUADS, 4, HD])
        q_pack = sb("q_pack", [P, QUADS, HEADS])
        k_pack = sb("k_pack", [P, QUADS, HEADS])
        v_pack = sb("v_pack", [P, QUADS, HEADS])
        s_shift = sb("s_shift", [P, QUADS, HEADS])
        s_exp = sb("s_exp", [P, QUADS, HEADS])
        s_keep = sb("s_keep", [P, QUADS, HEADS])
        probs = sb("probs", [P, QUADS, HEADS])
        probs_t = sb("probs_t", [P, QUADS, HEADS])
        s_max = sb("s_max", [P, QUADS])
        s_sum = sb("s_sum", [P, QUADS])
        s_inv = sb("s_inv", [P, QUADS])
        o_out = sb("o_out", [P, HEADS, SUB])
        tile_ps = [ctx.enter_context(nc.psum_tensor(f"tile_ps{s}", [P, CHUNK], F32)) for s in range(SLOTS)]
        scores_ps = ctx.enter_context(nc.psum_tensor("scores_ps", [P, QUADS, HEADS], F32))
        pv_ps = ctx.enter_context(nc.psum_tensor("pv_ps", [P, QUADS, HEADS], F32))

        bias_in = sem("bias_in")
        x_in = sem("x_in")
        x_hi_ready = sem("x_hi_ready")
        x_ready = sem("x_ready")
        w_in = [sem(f"w_in{s}") for s in range(SLOTS)]
        w_hi_ready = [sem(f"w_hi_ready{s}") for s in range(SLOTS)]
        w_ready = [sem(f"w_ready{s}") for s in range(SLOTS)]
        tile_done = [sem(f"tile_done{s}") for s in range(SLOTS)]
        tile_staged = [sem(f"tile_staged{s}") for s in range(SLOTS)]
        tile_stored = [sem(f"tile_stored{s}") for s in range(SLOTS)]
        half_in = [sem(f"half_in{h}") for h in range(2)]
        zeroed = sem("zeroed")
        qk_packed = sem("qk_packed")
        q_placed = sem("q_placed")
        v_copied = sem("v_copied")
        v_packed = sem("v_packed")
        scores_done = sem("scores_done")
        softmax_step = sem("softmax_step")
        exp_done = sem("exp_done")
        pv_done = sem("pv_done")
        o_copied = sem("o_copied")
        o_stored = sem("o_stored")

        block = ctx.enter_context(nc.Block())

        @block.sync
        def _(sp):
            sp.dma_start(x_raw[:], x_t[0]).then_inc(x_in, 16)
            sp.dma_start(bias[:], b_qkv).then_inc(bias_in, 16)
            for s in range(SLOTS):
                sp.dma_start(w_raw[s][:], w_qkv[s]).then_inc(w_in[s], 16)
            for s in range(SLOTS):
                sp.wait_ge(w_ready[s], 1)
                sp.dma_start(w_raw[s][:], w_qkv[SLOTS + s]).then_inc(w_in[s], 16)

            def iteration(chunk, it, load_tile):
                for s in range(SLOTS):
                    row = at(sp, (it - ITERS * chunk) * (SLOTS * P) + s * P)
                    weights = None if load_tile is None else at(sp, load_tile + s)
                    sp.wait_ge(tile_staged[s], it + 1)
                    sp.dma_start(qkv_dram[bass.ds(row, P), chunk * CHUNK:(chunk + 1) * CHUNK],
                                 stage[s][:]).then_inc(tile_stored[s], 16)
                    if load_tile is not None:
                        sp.wait_ge(w_ready[s], it + 2)
                        sp.dma_start(w_raw[s][:], w_qkv[weights]).then_inc(w_in[s], 16)

            for chunk in range(CHUNKS):
                first = chunk * ITERS
                loop(sp, first, ITERS - 2, lambda it: iteration(chunk, it, (it + 2 - first) * SLOTS))
                last = chunk == CHUNKS - 1
                if not last:
                    sp.wait_ge(x_ready, KT * (chunk + 1))
                    sp.dma_start(x_raw[:], x_t[chunk + 1]).then_inc(x_in, 16)
                for n in range(2):
                    iteration(chunk, first + ITERS - 2 + n, None if last else n * SLOTS)
            for s in range(SLOTS):
                sp.wait_ge(tile_stored[s], 16 * QKV_ITERS)

        @block.gpsimd
        def _(pool):
            nc.gpsimd.memset(q_diag[:], 0.0).then_inc(zeroed, 1)
            nc.gpsimd.memset(v_diag[:], 0.0).then_inc(zeroed, 1)
            pool.wait_ge(zeroed, 2)

            def load_half(chunk, half):
                if half == 0:
                    for s in range(SLOTS):
                        pool.wait_ge(tile_stored[s], 16 * ITERS * (chunk + 1))
                if chunk > 0:
                    used = BATCHES * (chunk - 1) + (half + 1) * BATCHES // 2
                    pool.wait_ge(qk_packed, 2 * used)
                    pool.wait_ge(v_copied, used)
                for n, dst in enumerate((q_in, k_in, v_in)):
                    for j in range(4):
                        t0 = chunk * CHUNK + j * SUB + half * HALF
                        src = qkv_dram[n * HID:(n + 1) * HID, t0:t0 + HALF].rearrange("(h d) t -> d h t", d=HD)
                        pool.dma_start(dst[32 * j:32 * j + 32, :, half * HALF:(half + 1) * HALF],
                                       src).then_inc(half_in[half], 16)

            def pack(chunk, i, half):
                b = chunk * BATCHES + i
                pool.wait_ge(half_in[half], LOADS_PER_HALF * (chunk + 1))
                pool.wait_ge(scores_done, b)
                t = bass.ds(i * QUADS, QUADS)
                nc.gpsimd.tensor_copy(q_pack[:], q_in[:, :, t].rearrange("p h t -> p t h")).then_inc(qk_packed, 1)
                nc.gpsimd.tensor_copy(k_pack[:], k_in[:, :, t].rearrange("p h t -> p t h")).then_inc(qk_packed, 1)
                pool.wait_ge(v_packed, b)
                nc.gpsimd.tensor_copy(v_pack[:], v_in[:, :, t].rearrange("p h t -> p t h")).then_inc(v_copied, 1)

            def store_o(chunk):
                pool.wait_ge(o_copied, BATCHES * (chunk + 1))
                for j in range(4):
                    t0 = chunk * CHUNK + j * SUB
                    dst = o_dram[:, t0:t0 + SUB].rearrange("(h d) t -> d h t", d=HD)
                    pool.dma_start(dst, o_out[32 * j:32 * j + 32, :, :]).then_inc(o_stored, 16)

            half = BATCHES // 2
            for chunk in range(CHUNKS + 1):
                if chunk < CHUNKS:
                    load_half(chunk, 0)
                if chunk > 0:
                    pack(chunk - 1, BATCHES - 1, 1)
                if chunk < CHUNKS:
                    load_half(chunk, 1)
                if chunk < CHUNKS:
                    pack(chunk, 0, 0)
                if chunk > 0:
                    store_o(chunk - 1)
                if chunk < CHUNKS:
                    loop(pool, 1, half - 1, lambda i: pack(chunk, i, 0))
                    loop(pool, half, half - 1, lambda i: pack(chunk, i, 1))
            pool.wait_ge(o_stored, 64 * CHUNKS)

        @block.scalar
        def _(act):
            def split_x(chunk):
                act.wait_ge(x_in, 16 * (chunk + 1))
                if chunk > 0:
                    for s in range(SLOTS):
                        act.wait_ge(tile_done[s], ITERS * chunk)
                for k in range(KT):
                    nc.scalar.copy(x_hi[:, k, :], x_raw[:, k, :]).then_inc(x_hi_ready, 1)

            def split_w(s, n):
                act.wait_ge(w_in[s], 16 * n + 16)
                act.wait_ge(tile_done[s], n)
                nc.scalar.copy(w_hi[s][:], w_raw[s][:]).then_inc(w_hi_ready[s], 1)

            def place_q(b):
                act.wait_ge(qk_packed, b * 2 + 1)
                act.wait_ge(scores_done, b)
                act.wait_ge(zeroed, 2)
                for j in range(4):
                    g = slice(32 * j, 32 * j + 32)
                    last = nc.scalar.copy(q_diag[g, :, j, :], q_pack[g, :, :])
                last.then_inc(q_placed, 1)

            def iteration(chunk, it, qkv, split, att, place):
                for s in range(SLOTS):
                    if qkv:
                        act.wait_ge(tile_done[s], it + 1)
                        act.wait_ge(tile_stored[s], 16 * it)
                        m = (it - ITERS * chunk) * SLOTS + s
                        nc.scalar.activation(stage[s][:], tile_ps[s][:], ACT.Identity,
                                             bias=bias[:, bass.ds(m, 1)]).then_inc(tile_staged[s], 1)
                    if split:
                        split_w(s, it + 1)
                    if att and s == 0:
                        b = it - LAG
                        act.wait_ge(softmax_step, b * SOFTMAX_STEPS + 2)
                        nc.scalar.activation(s_exp[:], s_shift[:], ACT.Exp, scale=scale).then_inc(exp_done, 1)
                    if place and s == 1:
                        place_q(it + 1 - LAG)
                if att:
                    b = it - LAG
                    act.wait_ge(pv_done, b + 1)
                    act.wait_ge(o_stored, (b // BATCHES) * 64)
                    t = bass.ds((b % BATCHES) * QUADS, QUADS)
                    nc.scalar.copy(o_out[:, :, t].rearrange("p h t -> p t h"), pv_ps[:]).then_inc(o_copied, 1)

            act.wait_ge(bias_in, 16)
            split_x(0)
            for s in range(SLOTS):
                split_w(s, 0)
            for first, count, chunk, new_x, qkv, split, att in SEGMENTS:
                if new_x:
                    split_x(chunk)
                if first == LAG:
                    place_q(0)
                if not qkv:
                    loop(act, first, count - 1, lambda it: iteration(chunk, it, qkv, split, att, True))
                    iteration(chunk, first + count - 1, qkv, split, att, False)
                else:
                    loop(act, first, count, lambda it: iteration(chunk, it, qkv, split, att, att))

        @block.vector
        def _(dve):
            def split_x(chunk):
                for k in range(KT):
                    dve.wait_ge(x_hi_ready, KT * chunk + k + 1)
                    nc.vector.tensor_tensor(x_lo[:, k, :], x_raw[:, k, :], x_hi[:, k, :].bitcast(F32),
                                            ALU.subtract).then_inc(x_ready, 1)

            def split_w(s, n):
                dve.wait_ge(w_hi_ready[s], n + 1)
                nc.vector.tensor_tensor(w_lo[s][:], w_raw[s][:], w_hi[s][:].bitcast(F32),
                                        ALU.subtract).then_inc(w_ready[s], 1)

            def iteration(chunk, it, qkv, split, att):
                b = it - LAG
                step = b * SOFTMAX_STEPS
                if att:
                    dve.wait_ge(scores_done, b + 1)
                    nc.vector.tensor_reduce(s_max[:], scores_ps[:], AX.X, ALU.max).then_inc(softmax_step, 1)
                    dve.wait_ge(softmax_step, step + 1)
                    nc.vector.tensor_tensor(s_shift[:], scores_ps[:],
                                            s_max[:].unsqueeze(2).to_broadcast([P, QUADS, HEADS]),
                                            ALU.subtract).then_inc(softmax_step, 1)
                    dve.wait_ge(v_copied, b + 1)
                    dve.wait_ge(pv_done, b)
                    dve.wait_ge(zeroed, 2)
                    for j in range(4):
                        g = slice(32 * j, 32 * j + 32)
                        last = nc.vector.transpose(v_diag[g, :, j, :], v_pack[g, :, :])
                    last.then_inc(v_packed, 1)
                if split:
                    split_w(0, it + 1)
                if att:
                    dve.wait_ge(exp_done, b + 1)
                    nc.vector.scalar_tensor_tensor(s_keep[:], scores_ps[:], threshold, s_exp[:],
                                                   ALU.is_gt, ALU.mult).then_inc(softmax_step, 1)
                    dve.wait_ge(softmax_step, step + 3)
                    nc.vector.tensor_reduce(s_sum[:], s_keep[:], AX.X, ALU.add).then_inc(softmax_step, 1)
                    dve.wait_ge(softmax_step, step + 4)
                    nc.vector.reciprocal(s_inv[:], s_sum[:]).then_inc(softmax_step, 1)
                    dve.wait_ge(softmax_step, step + 5)
                    nc.vector.tensor_tensor(probs[:], s_keep[:],
                                            s_inv[:].unsqueeze(2).to_broadcast([P, QUADS, HEADS]),
                                            ALU.mult).then_inc(softmax_step, 1)
                    dve.wait_ge(softmax_step, step + 6)
                    nc.vector.transpose(probs_t[:], probs[:]).then_inc(softmax_step, 1)
                if split:
                    split_w(1, it + 1)
                    split_w(2, it + 1)

            split_x(0)
            for s in range(SLOTS):
                split_w(s, 0)
            for first, count, chunk, new_x, qkv, split, att in SEGMENTS:
                if new_x:
                    split_x(chunk)
                loop(dve, first, count, lambda it: iteration(chunk, it, qkv, split, att))

        @block.tensor
        def _(pe):
            def tile(s):
                for k in range(KT):
                    for n, (w, x) in enumerate(((w_hi, x_hi), (w_hi, x_lo), (w_lo, x_hi))):
                        last = nc.tensor.matmul(tile_ps[s][:], w[s][:, k, :], x[:, k, :],
                                                start=(k == 0 and n == 0), stop=(k == KT - 1 and n == 2))
                last.then_inc(tile_done[s], 1)

            def iteration(chunk, it, qkv, split, att):
                b = it - LAG
                if att:
                    pe.wait_ge(qk_packed, b * 2 + 2)
                    pe.wait_ge(q_placed, b + 1)
                    pe.wait_ge(softmax_step, b * SOFTMAX_STEPS)
                    for t in range(QUADS):
                        last = nc.tensor.matmul(scores_ps[:, t, :], q_diag[:, t, :, :], k_pack[:, t, :],
                                                start=True, stop=True)
                    last.then_inc(scores_done, 1)
                if qkv:
                    pe.wait_ge(x_ready, KT * (chunk + 1))
                    for s in range(SLOTS):
                        pe.wait_ge(w_ready[s], it + 1)
                        pe.wait_ge(tile_staged[s], it)
                        tile(s)
                if att:
                    pe.wait_ge(v_packed, b + 1)
                    pe.wait_ge(softmax_step, (b + 1) * SOFTMAX_STEPS)
                    pe.wait_ge(o_copied, b)
                    for t in range(QUADS):
                        last = nc.tensor.matmul(pv_ps[:, t, :], v_diag[:, t, :, :], probs_t[:, t, :],
                                                start=True, stop=True)
                    last.then_inc(pv_done, 1)

            for first, count, chunk, new_x, qkv, split, att in SEGMENTS:
                loop(pe, first, count, lambda it: iteration(chunk, it, qkv, split, att))


SEGMENTS = [
    (0, ITERS, 0, False, True, True, False),
    (ITERS, LAG - ITERS, 1, True, True, True, False),
    (LAG, 2 * ITERS - LAG, 1, False, True, True, True),
    (2 * ITERS, ITERS, 2, True, True, True, True),
    (3 * ITERS, ITERS - 1, 3, True, True, True, True),
    (4 * ITERS - 1, 1, 3, False, True, False, True),
    (4 * ITERS, LAG, 4, False, False, False, True),
]


def projection_stage(nc, o_dram, w_o, b_o, x, identity, x1_dram, x1t_dram):
    with ExitStack() as ctx:
        def sb(name, shape, dt=F32):
            return ctx.enter_context(nc.sbuf_tensor(name, shape, dt))

        def sem(name):
            return ctx.enter_context(nc.semaphore(name))

        def pair(name, shape, dt=F32):
            return [sb(f"{name}{u}", shape, dt) for u in range(2)]

        ident = sb("ident", [P, P])
        bo = sb("bo", [P, HID])
        wo_raw = sb("wo_raw", [P, KT, HID])
        wo_hi = sb("wo_hi", [P, KT, HID], F32R)
        wo_lo = sb("wo_lo", [P, KT, HID], F32R)
        o_raw = pair("o_raw", [P, KT, P])
        o_hi = pair("o_hi", [P, KT, P], F32R)
        o_lo = pair("o_lo", [P, KT, P], F32R)
        x_tok = pair("x_tok", [P, HID])
        y = pair("y", [P, HID])
        x1 = pair("x1", [P, HID])
        x1t = pair("x1t", [P, KT, P])
        stats = pair("stats", [P, 2, 6])
        moments = pair("moments", [P, 2])
        root = pair("root", [P, 1])
        rstd = pair("rstd", [P, 1])
        eps = sb("eps", [P, 1])
        proj_ps = [ctx.enter_context(nc.psum_tensor(f"proj_ps{u}", [P, HID], F32)) for u in range(2)]
        turn_ps = [ctx.enter_context(nc.psum_tensor(f"turn_ps{u}", [P, KT, P], F32)) for u in range(2)]

        consts_in = sem("consts_in")
        eps_set = sem("eps_set")
        wo_in = sem("wo_in")
        wo_hi_ready = sem("wo_hi_ready")
        wo_ready = sem("wo_ready")
        o_in = [sem(f"o_in{u}") for u in range(2)]
        x_tok_in = [sem(f"x_tok_in{u}") for u in range(2)]
        o_hi_ready = [sem(f"o_hi_ready{u}") for u in range(2)]
        o_ready = [sem(f"o_ready{u}") for u in range(2)]
        proj_done = [sem(f"proj_done{u}") for u in range(2)]
        biased = [sem(f"biased{u}") for u in range(2)]
        norm_step = [sem(f"norm_step{u}") for u in range(2)]
        root_ready = [sem(f"root_ready{u}") for u in range(2)]
        turned = [sem(f"turned{u}") for u in range(2)]
        turned_copied = [sem(f"turned_copied{u}") for u in range(2)]
        x1_stored = [sem(f"x1_stored{u}") for u in range(2)]
        x1t_stored = [sem(f"x1t_stored{u}") for u in range(2)]
        NORM_STEPS = 7

        block = ctx.enter_context(nc.Block())
        per_chunk = FT // 2

        def pairs(eng, body):
            for chunk in range(FCHUNKS):
                def both(i):
                    for u in range(2):
                        body(chunk, i, u)
                loop(eng, chunk * per_chunk, per_chunk, both)

        @block.sync
        def _(sp):
            sp.dma_start(o_raw[0][:], o_dram[:, 0:P].rearrange("(k p) t -> p k t", p=P)).then_inc(o_in[0], 16)
            sp.dma_start(wo_raw[:], w_o).then_inc(wo_in, 16)
            sp.dma_start(ident[:], identity).then_inc(consts_in, 16)
            sp.dma_start(bo[:], b_o.partition_broadcast(P)).then_inc(consts_in, 16)
            sp.dma_start(x_tok[0][:], x[0:P, :]).then_inc(x_tok_in[0], 16)
            sp.dma_start(o_raw[1][:], o_dram[:, P:2 * P].rearrange("(k p) t -> p k t", p=P)).then_inc(o_in[1], 16)
            sp.dma_start(x_tok[1][:], x[P:2 * P, :]).then_inc(x_tok_in[1], 16)

            def tile(chunk, i, u, load=True):
                if load:
                    t = at(sp, i * (2 * P) + (2 + u) * P)
                    added = at(sp, i * NORM_STEPS + 1)
                    sp.wait_ge(o_ready[u], i + 1)
                    sp.dma_start(o_raw[u][:], o_dram[:, bass.ds(t, P)].rearrange("(k p) t -> p k t", p=P)
                                 ).then_inc(o_in[u], 16)
                    sp.wait_ge(norm_step[u], added)
                    sp.dma_start(x_tok[u][:], x[bass.ds(t, P), :]).then_inc(x_tok_in[u], 16)
                row = at(sp, i * (2 * P) + u * P)
                tile_no = at(sp, i * 2 + u)
                normed = at(sp, (i + 1) * NORM_STEPS)
                sp.wait_ge(norm_step[u], normed)
                sp.dma_start(x1_dram[bass.ds(row, P), :], x1[u][:]).then_inc(x1_stored[u], 16)
                sp.wait_ge(turned_copied[u], i + 1)
                sp.dma_start(x1t_dram[tile_no], x1t[u][:]).then_inc(x1t_stored[u], 16)

            for chunk in range(FCHUNKS):
                last = chunk == FCHUNKS - 1
                count = per_chunk - last

                def both(i):
                    for u in range(2):
                        tile(chunk, i, u)
                loop(sp, chunk * per_chunk, count, both)
                if last:
                    for u in range(2):
                        tile(chunk, OUT_TILES // 2 - 1, u, load=False)
            for u in range(2):
                sp.wait_ge(x1_stored[u], 16 * OUT_TILES // 2)
                sp.wait_ge(x1t_stored[u], 16 * OUT_TILES // 2)

        @block.gpsimd
        def _(pool):
            pool.wait_ge(consts_in, 32)

            def tile(chunk, i, u):
                pool.wait_ge(x_tok_in[u], 16 * i + 16)
                nc.gpsimd.tensor_tensor(x_tok[u][:], x_tok[u][:], bo[:], ALU.add).then_inc(biased[u], 1)
            pairs(pool, tile)

        @block.scalar
        def _(act):
            def split_o(u, n):
                act.wait_ge(o_in[u], 16 * n + 16)
                act.wait_ge(proj_done[u], n)
                nc.scalar.copy(o_hi[u][:], o_raw[u][:]).then_inc(o_hi_ready[u], 1)

            act.wait_ge(wo_in, 16)
            split_o(0, 0)
            for k in range(KT):
                nc.scalar.copy(wo_hi[:, k, :], wo_raw[:, k, :]).then_inc(wo_hi_ready, 1)
            split_o(1, 0)
            act.wait_ge(eps_set, 1)

            def tile(chunk, i, u, split=True):
                if split:
                    split_o(u, i + 1)
                act.wait_ge(norm_step[u], i * NORM_STEPS + 5)
                nc.scalar.activation(root[u][:], moments[u][:, 1:2], ACT.Sqrt, bias=eps[:]).then_inc(root_ready[u], 1)
                act.wait_ge(turned[u], i + 1)
                act.wait_ge(x1t_stored[u], 16 * i)
                nc.scalar.copy(x1t[u][:], turn_ps[u][:]).then_inc(turned_copied[u], 1)

            def both(chunk, split):
                def run(i):
                    for u in range(2):
                        tile(chunk, i, u, split)
                return run
            loop(act, 0, OUT_TILES // 2 - 1, both(0, True))
            loop(act, OUT_TILES // 2 - 1, 1, both(0, False))

        @block.vector
        def _(dve):
            def split_o(u, n):
                dve.wait_ge(o_hi_ready[u], n + 1)
                nc.vector.tensor_tensor(o_lo[u][:], o_raw[u][:], o_hi[u][:].bitcast(F32),
                                        ALU.subtract).then_inc(o_ready[u], 1)

            nc.vector.memset(eps[:], EPS).then_inc(eps_set, 1)
            split_o(0, 0)
            for k in range(KT):
                dve.wait_ge(wo_hi_ready, k + 1)
                nc.vector.tensor_tensor(wo_lo[:, k, :], wo_raw[:, k, :], wo_hi[:, k, :].bitcast(F32),
                                        ALU.subtract).then_inc(wo_ready, 1)
            split_o(1, 0)

            def tile(i, u, split):
                step = i * NORM_STEPS
                dve.wait_ge(proj_done[u], i + 1)
                dve.wait_ge(biased[u], i + 1)
                nc.vector.tensor_tensor(y[u][:], proj_ps[u][:], x_tok[u][:], ALU.add).then_inc(norm_step[u], 1)
                dve.wait_ge(norm_step[u], step + 1)
                for n in range(2):
                    nc.vector.bn_stats(stats[u][:, n, :], y[u][:, n * 512:(n + 1) * 512]).then_inc(norm_step[u], 1)
                if split:
                    split_o(u, i + 1)
                dve.wait_ge(norm_step[u], step + 3)
                nc.vector.bn_aggr(moments[u][:], stats[u][:]).then_inc(norm_step[u], 2)
                dve.wait_ge(root_ready[u], i + 1)
                nc.vector.reciprocal(rstd[u][:], root[u][:]).then_inc(norm_step[u], 1)
                dve.wait_ge(norm_step[u], step + 6)
                dve.wait_ge(x1_stored[u], 16 * i)
                dve.wait_ge(turned[u], i)
                nc.vector.tensor_scalar(x1[u][:], y[u][:], moments[u][:, 0:1], rstd[u][:],
                                        ALU.subtract, ALU.mult).then_inc(norm_step[u], 1)

            def both(split):
                def run(i):
                    for u in range(2):
                        tile(i, u, split)
                return run
            loop(dve, 0, OUT_TILES // 2 - 1, both(True))
            loop(dve, OUT_TILES // 2 - 1, 1, both(False))

        @block.tensor
        def _(pe):
            pe.wait_ge(consts_in, 32)
            pe.wait_ge(wo_ready, KT)

            def project(i, u):
                pe.wait_ge(o_ready[u], i + 1)
                pe.wait_ge(norm_step[u], i * NORM_STEPS)
                for k in range(KT):
                    for m, (o, w) in enumerate(((o_hi, wo_hi), (o_hi, wo_lo), (o_lo, wo_hi))):
                        for n in range(2):
                            last = nc.tensor.matmul(proj_ps[u][:, n * 512:(n + 1) * 512], o[u][:, k, :],
                                                    w[:, k, n * 512:(n + 1) * 512],
                                                    start=(k == 0 and m == 0), stop=(k == KT - 1 and m == 2))
                last.then_inc(proj_done[u], 1)

            def turn(i, u):
                pe.wait_ge(norm_step[u], (i + 1) * NORM_STEPS)
                pe.wait_ge(turned_copied[u], i)
                for k in range(KT):
                    last = nc.tensor.transpose(turn_ps[u][:, k, :], x1[u][:, k * P:(k + 1) * P], ident[:])
                last.then_inc(turned[u], 1)

            project(0, 0)

            def both(i):
                project(i, 1)
                turn(i, 0)
                project(i + 1, 0)
                turn(i, 1)
            loop(pe, 0, OUT_TILES // 2 - 1, both)
            project(OUT_TILES // 2 - 1, 1)
            turn(OUT_TILES // 2 - 1, 0)
            turn(OUT_TILES // 2 - 1, 1)


def feed_forward_stage(nc, chunk, x1t_dram, w_gu, w_d, x1_dram, identity_bf, out):
    with ExitStack() as ctx:
        inner = ctx.enter_context(nc.sbuf_tensor(f"inner{chunk}", [P, ICH, FCH], F32R))
        gate_up(nc, chunk, x1t_dram, w_gu, inner)
        down(nc, chunk, w_d, x1_dram, identity_bf, inner, out)


TRUNC_STEPS = 5


def gate_up(nc, chunk, x1t_dram, w_gu, inner):
    with ExitStack() as ctx:
        def sb(name, shape, dt=F32):
            return ctx.enter_context(nc.sbuf_tensor(f"{name}_g{chunk}", shape, dt))

        def sem(name):
            return ctx.enter_context(nc.semaphore(f"{name}_g{chunk}"))

        xt_hi = sb("xt_hi", [P, KT, FCH], F32R)
        xt_lo = sb("xt_lo", [P, KT, FCH], F32R)
        w_raw = [sb(f"gw_raw{u}", [P, KT, P]) for u in range(2)]
        w_hi = [sb(f"gw_hi{u}", [P, KT, P], F32R) for u in range(2)]
        w_lo = [sb(f"gw_lo{u}", [P, KT, P], F32R) for u in range(2)]
        silu = sb("silu", [P, FCH])
        val = sb("val", [P, FCH])
        mag = sb("mag", [P, FCH])
        sign = sb("sign", [P, FCH])
        near = sb("near", [P, FCH])
        xt_raw = [val, mag]
        gate_ps = ctx.enter_context(nc.psum_tensor(f"gate_ps{chunk}", [P, FCH], F32))
        up_ps = ctx.enter_context(nc.psum_tensor(f"up_ps{chunk}", [P, FCH], F32))
        ps = [gate_ps, up_ps]

        xt_in = [sem(f"xt_in{u}") for u in range(2)]
        xt_hi_ready = sem("xt_hi_ready")
        xt_ready = sem("xt_ready")
        w_in = [sem(f"w_in{u}") for u in range(2)]
        w_hi_ready = [sem(f"w_hi_ready{u}") for u in range(2)]
        w_ready = [sem(f"w_ready{u}") for u in range(2)]
        done = [sem("gate_done"), sem("up_done")]
        silu_ready = sem("silu_ready")
        rest_up_ready = sem("rest_up_ready")
        product = sem("product")
        clipped = sem("clipped")
        mag_ready = sem("mag_ready")
        sign_ready = sem("sign_ready")
        trunc_step = sem("trunc_step")
        rest_copied = sem("rest_copied")

        block = ctx.enter_context(nc.Block())

        @block.sync
        def _(sp):
            for u in range(2):
                sp.dma_start(w_raw[u][:], w_gu[u]).then_inc(w_in[u], 16)
                sp.dma_start(xt_raw[u][:].rearrange("p (n t) -> p n t", t=P), x1t_dram[chunk * FT:(chunk + 1) * FT, :, u, :].rearrange("n p t -> p n t")).then_inc(xt_in[u], 16)
            for k in range(2, KT):
                sp.wait_ge(xt_ready, k - 1)
                sp.dma_start(xt_raw[k % 2][:].rearrange("p (n t) -> p n t", t=P),
                             x1t_dram[chunk * FT:(chunk + 1) * FT, :, k, :].rearrange("n p t -> p n t")).then_inc(xt_in[k % 2], 16)

            def load(n):
                for u in range(2):
                    weights = at(sp, n * 2 + u)
                    sp.wait_ge(w_ready[u], n)
                    sp.dma_start(w_raw[u][:], w_gu[weights]).then_inc(w_in[u], 16)
            loop(sp, 1, GTILES - 1, load)
            sp.wait_ge(w_ready[0], GTILES)
            sp.dma_start(w_raw[0][:], w_gu[2 * GTILES]).then_inc(w_in[0], 16)

        @block.gpsimd
        def _(pool):
            pass

        @block.scalar
        def _(act):
            def split_w(u, n):
                act.wait_ge(w_in[u], 16 * n + 16)
                act.wait_ge(done[u], n)
                nc.scalar.copy(w_hi[u][:], w_raw[u][:]).then_inc(w_hi_ready[u], 1)

            split_w(0, 0)
            for k in range(KT):
                act.wait_ge(xt_in[k % 2], 16 * (k // 2) + 16)
                nc.scalar.copy(xt_hi[:, k, :], xt_raw[k % 2][:]).then_inc(xt_hi_ready, 1)
            split_w(1, 0)

            def tile(n, rows, next_up):
                act.wait_ge(done[0], n + 1)
                act.wait_ge(product, n)
                nc.scalar.activation(silu[0:rows, :], gate_ps[0:rows, :], ACT.Silu,
                                     scale=1.0 / 128.0).then_inc(silu_ready, 1)
                if rows < P:
                    nc.scalar.copy(near[0:rows, :], gate_ps[rows:2 * rows, :]).then_inc(rest_up_ready, 1)
                else:
                    split_w(0, n + 1)
                if next_up:
                    split_w(1, n + 1)
                act.wait_ge(clipped, n + 1)
                nc.scalar.activation(mag[0:rows, :], val[0:rows, :], ACT.Abs).then_inc(mag_ready, 1)
                nc.scalar.activation(sign[0:rows, :], val[0:rows, :], ACT.Sign, scale=-1.0).then_inc(sign_ready, 1)

            act.wait_ge(xt_ready, KT)
            loop(act, 0, GTILES - 1, lambda n: tile(n, P, True))
            tile(GTILES - 1, P, False)
            act.wait_ge(trunc_step, GTILES * TRUNC_STEPS)
            tile(GTILES, REST, False)
            act.wait_ge(trunc_step, ICH * TRUNC_STEPS)
            nc.scalar.copy(inner[REST:2 * REST, GTILES, :], inner[0:REST, GTILES, :].bitcast(F32)
                           ).then_inc(rest_copied, 1)

        @block.vector
        def _(dve):
            def split_w(u, n):
                dve.wait_ge(w_hi_ready[u], n + 1)
                nc.vector.tensor_tensor(w_lo[u][:], w_raw[u][:], w_hi[u][:].bitcast(F32),
                                        ALU.subtract).then_inc(w_ready[u], 1)

            split_w(0, 0)
            for k in range(KT):
                dve.wait_ge(xt_hi_ready, k + 1)
                nc.vector.tensor_tensor(xt_lo[:, k, :], xt_raw[k % 2][:], xt_hi[:, k, :].bitcast(F32),
                                        ALU.subtract).then_inc(xt_ready, 1)
            split_w(1, 0)
            dve.wait_ge(xt_ready, KT)

            def tile(n, rows, next_up):
                r = slice(0, rows)
                step = n * TRUNC_STEPS
                if rows == P:
                    split_w(0, n + 1)
                dve.wait_ge(silu_ready, n + 1)
                dve.wait_ge(sign_ready, n)
                if rows == P:
                    dve.wait_ge(done[1], n + 1)
                    nc.vector.tensor_tensor(val[r, :], up_ps[r, :], silu[r, :], ALU.mult).then_inc(product, 1)
                else:
                    dve.wait_ge(rest_up_ready, 1)
                    nc.vector.tensor_tensor(val[r, :], near[r, :], silu[r, :], ALU.mult).then_inc(product, 1)
                dve.wait_ge(product, n + 1)
                nc.vector.tensor_scalar(val[r, :], val[r, :], -128.0, 127.0, ALU.max, ALU.min).then_inc(clipped, 1)
                if next_up:
                    split_w(1, n + 1)
                dve.wait_ge(mag_ready, n + 1)
                nc.vector.tensor_scalar(near[r, :], mag[r, :], ROUND, ROUND, ALU.add, ALU.subtract
                                        ).then_inc(trunc_step, 1)
                dve.wait_ge(trunc_step, step + 1)
                nc.vector.tensor_tensor(mag[r, :], near[r, :], mag[r, :], ALU.is_gt).then_inc(trunc_step, 1)
                dve.wait_ge(trunc_step, step + 2)
                nc.vector.tensor_tensor(near[r, :], mag[r, :], near[r, :], ALU.subtract).then_inc(trunc_step, 1)
                dve.wait_ge(trunc_step, step + 3)
                dve.wait_ge(sign_ready, n + 1)
                nc.vector.tensor_tensor(inner[r, bass.ds(n, 1), :].rearrange("p a t -> p (a t)"), near[r, :],
                                        sign[r, :], ALU.mult).then_inc(trunc_step, 2)

            loop(dve, 0, GTILES - 1, lambda n: tile(n, P, True))
            tile(GTILES - 1, P, False)
            tile(GTILES, REST, False)

        @block.tensor
        def _(pe):
            def tile(u, n):
                pe.wait_ge(w_ready[u], n + 1)
                if u == 0:
                    pe.wait_ge(silu_ready, n)
                else:
                    pe.wait_ge(product, n)
                for k in range(KT):
                    for m, (w, x) in enumerate(((w_hi, xt_hi), (w_hi, xt_lo), (w_lo, xt_hi))):
                        for h in range(2):
                            last = nc.tensor.matmul(ps[u][:, h * 512:(h + 1) * 512], w[u][:, k, :],
                                                    x[:, k, h * 512:(h + 1) * 512],
                                                    start=(k == 0 and m == 0), stop=(k == KT - 1 and m == 2))
                last.then_inc(done[u], 1)

            pe.wait_ge(xt_ready, KT)

            def both(n):
                tile(0, n)
                tile(1, n)
            loop(pe, 0, GTILES, both)
            tile(0, GTILES)


def down(nc, chunk, w_d, x1_dram, identity_bf, inner, out):
    with ExitStack() as ctx:
        def sb(name, shape, dt=F32):
            return ctx.enter_context(nc.sbuf_tensor(f"{name}_d{chunk}", shape, dt))

        def sem(name):
            return ctx.enter_context(nc.semaphore(f"{name}_d{chunk}"))

        ident = sb("ident_bf", [P, P], BF16)
        w_raw = sb("dw_raw", [P, ICH, P])
        w_hi = [sb(f"dw_hi{u}", [P, ICH, P], F32R) for u in range(2)]
        w_lo = [sb(f"dw_lo{u}", [P, ICH, P], F32R) for u in range(2)]
        y = sb("y", [P, FT, HID])
        val = sb("val", [P, FCH])
        near = sb("near", [P, FCH])
        sign = sb("sign", [P, FCH])
        quant = sb("quant", [P, FCH], BF16)
        stats = sb("stats", [P, FT, KT, 6])
        moments = sb("moments", [P, FT, 2])
        root = sb("root", [P, FT])
        rstd = sb("rstd", [P, FT])
        eps = sb("eps2", [P, 1])
        down_ps = [ctx.enter_context(nc.psum_tensor(f"down_ps{chunk}{u}", [P, FCH], F32)) for u in range(2)]
        turn_ps = ctx.enter_context(nc.psum_tensor(f"turnd_ps{chunk}", [P, FT, P], BF16))

        consts_in = sem("consts_in")
        y_in = sem("y_in")
        eps_set = sem("eps_set")
        w_in = sem("w_in")
        w_hi_ready = [sem(f"w_hi_ready{u}") for u in range(2)]
        w_ready = [sem(f"w_ready{u}") for u in range(2)]
        w_rest = [sem(f"w_rest{u}") for u in range(2)]
        done = [sem(f"done{u}") for u in range(2)]
        scaled = sem("scaled")
        clipped = sem("clipped")
        mag_ready = sem("mag_ready")
        sign_ready = sem("sign_ready")
        trunc_step = sem("trunc_step")
        turned = sem("turned")
        added = sem("added")
        counted = sem("counted")
        moments_ready = sem("moments_ready")
        root_ready = sem("root_ready")
        rstd_ready = sem("rstd_ready")
        normed = sem("normed")
        stored = sem("stored")

        block = ctx.enter_context(nc.Block())
        pairs = KT // 2

        @block.sync
        def _(sp):
            sp.dma_start(w_raw[:], w_d[0]).then_inc(w_in, 16)
            sp.dma_start(ident[:], identity_bf).then_inc(consts_in, 16)
            sp.dma_start(y[:], x1_dram[chunk * FCH:(chunk + 1) * FCH, :].rearrange("(t p) c -> p t c", p=P)
                         ).then_inc(y_in, 16)

            def load(i, u):
                weights = at(sp, i * 2 + u)
                sp.wait_ge(w_ready[1 - u], i + u)
                sp.dma_start(w_raw[:], w_d[weights]).then_inc(w_in, 16)
            load(0, 1)

            def both(i):
                load(i, 0)
                load(i, 1)
            loop(sp, 1, pairs - 1, both)
            for t in range(FT):
                sp.wait_ge(normed, t + 1)
                row = chunk * FCH + t * P
                sp.dma_start(out[row:row + P, :], y[:, t, :]).then_inc(stored, 16)
            sp.wait_ge(stored, 16 * FT)

        @block.gpsimd
        def _(pool):
            pass

        @block.scalar
        def _(act):
            def split_w(i, u):
                act.wait_ge(w_in, i * 32 + u * 16 + 16)
                act.wait_ge(done[u], i)
                nc.scalar.copy(w_hi[u][:], w_raw[:]).then_inc(w_hi_ready[u], 1)

            def quantise(i, u):
                n = i * 2 + u
                act.wait_ge(done[u], i + 1)
                act.wait_ge(trunc_step, n * TRUNC_STEPS)
                nc.scalar.mul(val[:], down_ps[u][:], 128.0).then_inc(scaled, 1)
                act.wait_ge(clipped, n + 1)
                nc.scalar.activation(sign[:], val[:], ACT.Sign, scale=-1.0).then_inc(sign_ready, 1)
                act.wait_ge(sign_ready, n + 1)
                nc.scalar.activation(val[:], val[:], ACT.Abs).then_inc(mag_ready, 1)

            split_w(0, 0)
            split_w(0, 1)

            def both(i):
                quantise(i, 0)
                split_w(i + 1, 0)
                quantise(i, 1)
                split_w(i + 1, 1)
            loop(act, 0, pairs - 1, both)
            quantise(pairs - 1, 0)
            quantise(pairs - 1, 1)
            act.wait_ge(eps_set, 1)
            act.wait_ge(moments_ready, FT)
            nc.scalar.activation(root[:], moments[:, :, 1], ACT.Sqrt, bias=eps[:]).then_inc(root_ready, 1)

        @block.vector
        def _(dve):
            nc.vector.memset(eps[:], EPS).then_inc(eps_set, 1)

            def split_w(i, u):
                dve.wait_ge(w_hi_ready[u], i + 1)
                rest = slice(REST, 2 * REST)
                nc.vector.tensor_tensor(w_lo[u][:, 0:GTILES, :], w_raw[:, 0:GTILES, :],
                                        w_hi[u][:, 0:GTILES, :].bitcast(F32), ALU.subtract).then_inc(w_rest[u], 1)
                nc.vector.tensor_tensor(w_hi[u][rest, GTILES, :], w_raw[rest, GTILES, :],
                                        w_hi[u][rest, GTILES, :].bitcast(F32), ALU.subtract).then_inc(w_ready[u], 1)

            def quantise(i, u):
                n = i * 2 + u
                step = n * TRUNC_STEPS
                dve.wait_ge(scaled, n + 1)
                nc.vector.tensor_scalar(val[:], val[:], -128.0, 127.0, ALU.max, ALU.min).then_inc(clipped, 1)
                dve.wait_ge(mag_ready, n + 1)
                nc.vector.tensor_scalar(near[:], val[:], ROUND, ROUND, ALU.add, ALU.subtract).then_inc(trunc_step, 1)
                dve.wait_ge(trunc_step, step + 1)
                nc.vector.tensor_tensor(val[:], near[:], val[:], ALU.is_gt).then_inc(trunc_step, 1)
                dve.wait_ge(trunc_step, step + 2)
                nc.vector.tensor_tensor(near[:], val[:], near[:], ALU.subtract).then_inc(trunc_step, 1)
                dve.wait_ge(trunc_step, step + 3)
                dve.wait_ge(turned, n)
                nc.vector.tensor_tensor(quant[:], near[:], sign[:], ALU.mult).then_inc(trunc_step, 2)

            def add(i, u):
                n = i * 2 + u
                dve.wait_ge(turned, n + 1)
                c = bass.ds(n * P, P)
                nc.vector.tensor_tensor(y[:, :, c], turn_ps[:], y[:, :, c], ALU.add).then_inc(added, 1)
                dve.wait_ge(added, n + 1)
                for t in range(FT):
                    last = nc.vector.bn_stats(stats[:, t, bass.ds(n, 1), :].rearrange("p a s -> p (a s)"), y[:, t, c])
                last.then_inc(counted, 1)

            split_w(0, 0)
            split_w(0, 1)
            dve.wait_ge(y_in, 16)
            quantise(0, 0)
            split_w(1, 0)

            def both(i):
                quantise(i, 1)
                add(i, 0)
                split_w(i + 1, 1)
                quantise(i + 1, 0)
                add(i, 1)
                split_w(i + 2, 0)
            loop(dve, 0, pairs - 2, both)
            i = pairs - 2
            quantise(i, 1)
            add(i, 0)
            split_w(i + 1, 1)
            quantise(i + 1, 0)
            add(i, 1)
            quantise(i + 1, 1)
            add(i + 1, 0)
            add(i + 1, 1)
            dve.wait_ge(counted, KT)
            for t in range(FT):
                nc.vector.bn_aggr(moments[:, t, :], stats[:, t, :, :]).then_inc(moments_ready, 1)
            dve.wait_ge(root_ready, 1)
            nc.vector.reciprocal(rstd[:], root[:]).then_inc(rstd_ready, 1)
            dve.wait_ge(rstd_ready, 1)
            for t in range(FT):
                nc.vector.tensor_scalar(y[:, t, :], y[:, t, :], moments[:, t, 0:1], rstd[:, t:t + 1],
                                        ALU.subtract, ALU.mult).then_inc(normed, 1)

        @block.tensor
        def _(pe):
            def tile(i, u):
                pe.wait_ge(w_ready[u], i + 1)
                pe.wait_ge(scaled, i * 2 + u if isinstance(i, int) and i == 0 else i * 2 + u - 1)
                for c in range(ICH):
                    for m, w in enumerate((w_hi, w_lo)):
                        if c == GTILES and m == 1:
                            continue
                        for h in range(2):
                            last = nc.tensor.matmul(down_ps[u][:, h * 512:(h + 1) * 512], w[u][:, c, :],
                                                    inner[:, c, h * 512:(h + 1) * 512],
                                                    start=(c == 0 and m == 0), stop=(c == GTILES))
                last.then_inc(done[u], 1)

            def turn(i, u):
                n = i * 2 + u
                pe.wait_ge(trunc_step, (n + 1) * TRUNC_STEPS)
                pe.wait_ge(added, n)
                for t in range(FT):
                    last = nc.tensor.transpose(turn_ps[:, t, :], quant[:, t * P:(t + 1) * P], ident[:])
                last.then_inc(turned, 1)

            pe.wait_ge(consts_in, 16)
            tile(0, 0)

            def both(i):
                tile(i, 1)
                turn(i, 0)
                tile(i + 1, 0)
                turn(i, 1)
            loop(pe, 0, pairs - 1, both)
            tile(pairs - 1, 1)
            turn(pairs - 1, 0)
            turn(pairs - 1, 1)


def build(nc, ins, out):
    qkv_dram = nc.dram_tensor("qkv_scratch", (3 * HID, TOKENS), F32).ap()
    o_dram = nc.dram_tensor("o_scratch", (HID, TOKENS), F32).ap()
    x1_dram = nc.dram_tensor("x1_scratch", (TOKENS, HID), F32).ap()
    x1t_dram = nc.dram_tensor("x1t_scratch", (OUT_TILES, P, KT, P), F32).ap()
    attention_stage(nc, ins["x_t"], ins["w_qkv"], ins["b_qkv"], qkv_dram, o_dram)
    projection_stage(nc, o_dram, ins["w_o"], ins["b_o"], ins["x"], ins["identity"], x1_dram, x1t_dram)
    for chunk in range(FCHUNKS):
        feed_forward_stage(nc, chunk, x1t_dram, ins["w_gu"], ins["w_d"], x1_dram, ins["identity_bf"], out)


def kernel(L0_attn_x, L0_attn_Wq, L0_attn_bq, L0_attn_Wk, L0_attn_bk, L0_attn_Wv, L0_attn_bv, L0_attn_Wo,
           L0_attn_bo, L0_ffn_w_gate, L0_ffn_w_up, L0_ffn_w_down):
    import ml_dtypes
    import concourse.bacc as bacc
    from concourse.bass_utils import run_bass_kernel_spmd

    shape = L0_attn_x.shape
    x = np.ascontiguousarray(L0_attn_x).reshape(TOKENS, HID)

    def tiles(w):
        return np.asarray(w).reshape(-1, P, KT, P).transpose(0, 3, 2, 1)

    gate, up = np.asarray(L0_ffn_w_gate), np.asarray(L0_ffn_w_up)
    whole = GTILES * P
    pairs = np.stack([tiles(gate[:whole]), tiles(up[:whole])], axis=1).reshape(2 * GTILES, P, KT, P)
    rest = tiles(np.concatenate([gate[whole:], up[whole:]]))
    wd = np.asarray(L0_ffn_w_down)
    wd = np.concatenate([wd, wd[:, whole:]], axis=1).reshape(KT, P, ICH, P).transpose(0, 3, 2, 1)
    arrays = {
        "x": x,
        "x_t": x.reshape(CHUNKS, CHUNK, KT, P).transpose(0, 3, 2, 1),
        "w_qkv": tiles(np.concatenate([L0_attn_Wq, L0_attn_Wk, L0_attn_Wv])),
        "b_qkv": np.concatenate([L0_attn_bq, L0_attn_bk, L0_attn_bv]).reshape(QKV_TILES, P).T,
        "w_o": np.asarray(L0_attn_Wo).reshape(HID, KT, P).transpose(2, 1, 0),
        "b_o": np.asarray(L0_attn_bo),
        "identity": np.eye(P, dtype=np.float32),
        "identity_bf": np.eye(P, dtype=ml_dtypes.bfloat16),
        "w_gu": np.concatenate([pairs, rest]),
        "w_d": wd,
    }
    nc = bacc.Bacc("TRN2", target_bir_lowering=False, num_devices=1)
    arrays = {n: np.ascontiguousarray(a) for n, a in arrays.items()}
    ins = {n: nc.dram_tensor(f"in_{n}", a.shape, mybir.dt.from_np(a.dtype), kind="ExternalInput").ap()
           for n, a in arrays.items()}
    out = nc.dram_tensor("out", (TOKENS, HID), F32, kind="ExternalOutput").ap()
    build(nc, ins, out)
    run = run_bass_kernel_spmd(nc, [{f"in_{n}": a for n, a in arrays.items()}], core_ids=[0])
    return run.results[0]["out"].reshape(shape)
```

```python
from contextlib import ExitStack

import numpy as np

import concourse.bass as bass
from concourse import mybir
from concourse.alu_op_type import AluOpType as ALU

F32 = mybir.dt.float32
F32R = mybir.dt.float32r
BF16 = mybir.dt.bfloat16
ACT = mybir.ActivationFunctionType
AX = mybir.AxisListType

P = 128
TOKENS = 2048
HID = 1024
KT = HID // P
HEADS = 32
HD = HID // HEADS
INTER = 2752
EPS = 1e-5

CHUNK = 512
CHUNKS = TOKENS // CHUNK
SUB = CHUNK // 4
SLOTS = 3
QKV_TILES = 3 * HID // P
ITERS = QKV_TILES // SLOTS
QUADS = 16
BATCHES = SUB // QUADS
HALF = SUB // 2
LAG = ITERS + 2
QKV_ITERS = CHUNKS * ITERS
ATT_BATCHES = CHUNKS * BATCHES
TAIL = QKV_ITERS - LAG
LOADS_PER_HALF = 3 * 4 * 16
SOFTMAX_STEPS = 6
NORM_STEPS = 7
TRUNC_STEPS = 5

FCH = 1024
FCHUNKS = TOKENS // FCH
FT = FCH // P
GTILES = INTER // P
REST = INTER - GTILES * P
ICH = GTILES + 1
PIECE = ICH // 2
ROUND = 1.5 * 2.0**23
OUT_TILES = TOKENS // P


def score_scale():
    return np.float32(1.0 / np.sqrt(HD))


def raw_threshold():
    scale, limit = score_scale(), np.float32(0.001)
    s = np.float32(limit / scale)
    while np.float32(s * scale) > limit:
        s = np.nextafter(s, np.float32(0), dtype=np.float32)
    while np.float32(np.nextafter(s, np.float32(1), dtype=np.float32) * scale) <= limit:
        s = np.nextafter(s, np.float32(1), dtype=np.float32)
    return float(s)


def loop(eng, first, count, body):
    if count == 1:
        body(first)
    else:
        with eng.Fori(first, first + count) as i:
            body(i)


def at(eng, value):
    return value if isinstance(value, int) else eng.snap(value)


def attention_stage(nc, sems, x_t, w_qkv, b_qkv, identity, qkv_dram, o_dram):
    scale, threshold = float(score_scale()), raw_threshold()
    with ExitStack() as ctx:
        def sb(name, shape, dt=F32):
            return ctx.enter_context(nc.sbuf_tensor(name, shape, dt))

        def sem(name):
            return sems.enter_context(nc.semaphore(name))

        bias = sb("bias", [P, QKV_TILES])
        ident = sb("ident1", [P, P])
        x_raw = sb("x_raw", [P, KT, CHUNK])
        x_hi = sb("x_hi", [P, KT, CHUNK], F32R)
        x_lo = sb("x_lo", [P, KT, CHUNK], F32R)
        w_raw = [sb(f"w_raw{s}", [P, KT, P]) for s in range(SLOTS)]
        w_hi = [sb(f"w_hi{s}", [P, KT, P], F32R) for s in range(SLOTS)]
        w_lo = [sb(f"w_lo{s}", [P, KT, P], F32R) for s in range(SLOTS)]
        stage = [sb(f"stage{s}", [P, CHUNK]) for s in range(SLOTS)]
        q_in = sb("q_in", [P, HEADS, SUB])
        k_in = sb("k_in", [P, HEADS, SUB])
        v_in = sb("v_in", [P, HEADS, SUB])
        k_diag = sb("k_diag", [P, QUADS, 4, HEADS])
        v_diag = sb("v_diag", [P, QUADS, 4, HD])
        q_pack = sb("q_pack", [P, QUADS, HEADS])
        v_pack = sb("v_pack", [P, QUADS, HEADS])
        s_shift = sb("s_shift", [P, QUADS, HEADS])
        s_exp = sb("s_exp", [P, QUADS, HEADS])
        s_keep = sb("s_keep", [P, QUADS, HEADS])
        probs = sb("probs", [P, QUADS, HEADS])
        probs_t = sb("probs_t", [P, QUADS, HEADS])
        o_rows = sb("o_rows", [P, QUADS, HD])
        s_max = sb("s_max", [P, QUADS])
        s_sum = sb("s_sum", [P, QUADS])
        s_inv = sb("s_inv", [P, QUADS])
        o_out = sb("o_out", [P, HEADS, SUB])
        tile_ps = [ctx.enter_context(nc.psum_tensor(f"tile_ps{s}", [P, CHUNK], F32)) for s in range(SLOTS)]
        scores_ps = ctx.enter_context(nc.psum_tensor("scores_ps", [P, QUADS, HEADS], F32))
        pv_ps = ctx.enter_context(nc.psum_tensor("pv_ps", [P, QUADS, HD], F32))
        probs_ps = ctx.enter_context(nc.psum_tensor("probs_ps", [P, QUADS, HEADS], F32))
        o_ps = ctx.enter_context(nc.psum_tensor("o_ps", [P, QUADS, HEADS], F32))

        bias_in = sem("bias_in")
        x_in = sem("x_in")
        x_piece_in = [sem(f"x_piece_in{k}") for k in range(KT)]
        x_hi_ready = sem("x_hi_ready")
        x_ready = sem("x_ready")
        w_in = [sem(f"qkv_w_in{s}") for s in range(SLOTS)]
        w_hi_ready = [sem(f"qkv_w_hi_ready{s}") for s in range(SLOTS)]
        w_ready = [sem(f"qkv_w_ready{s}") for s in range(SLOTS)]
        tile_done = [sem(f"tile_done{s}") for s in range(SLOTS)]
        tile_staged = [sem(f"tile_staged{s}") for s in range(SLOTS)]
        tile_stored = [sem(f"tile_stored{s}") for s in range(SLOTS)]
        half_in = [sem(f"half_in{h}") for h in range(2)]
        zeroed = sem("zeroed")
        q_packed = sem("q_packed")
        k_placed = sem("k_placed")
        v_copied = sem("v_copied")
        v_packed = sem("v_packed")
        scores_done = sem("scores_done")
        softmax_step = sem("softmax_step")
        exp_done = sem("exp_done")
        probs_turned = sem("probs_turned")
        probs_copied = sem("probs_copied")
        pv_done = sem("pv_done")
        pv_copied = sem("pv_copied")
        o_turned = sem("o_turned")
        o_copied = sem("o_copied")
        o_stored = sem("o_stored")

        block = ctx.enter_context(nc.Block())

        @block.sync
        def _(sp):
            sp.dma_start(w_raw[0][:], w_qkv[0]).then_inc(w_in[0], 16)
            for k in range(KT):
                sp.dma_start(x_raw[:, k, :], x_t[0, :, k, :]).then_inc(x_piece_in[k], 16)
            for s in range(1, SLOTS):
                sp.dma_start(w_raw[s][:], w_qkv[s]).then_inc(w_in[s], 16)
            sp.dma_start(bias[:], b_qkv).then_inc(bias_in, 16)
            sp.dma_start(ident[:], identity).then_inc(bias_in, 16)
            for s in range(SLOTS):
                sp.wait_ge(w_ready[s], 1)
                sp.dma_start(w_raw[s][:], w_qkv[SLOTS + s]).then_inc(w_in[s], 16)

            def iteration(chunk, it, load_tile):
                for s in range(SLOTS):
                    row = at(sp, (it - ITERS * chunk) * (SLOTS * P) + s * P)
                    weights = None if load_tile is None else at(sp, load_tile + s)
                    sp.wait_ge(tile_staged[s], it + 1)
                    sp.dma_start(qkv_dram[bass.ds(row, P), chunk * CHUNK:(chunk + 1) * CHUNK],
                                 stage[s][:]).then_inc(tile_stored[s], 16)
                    if load_tile is not None:
                        sp.wait_ge(w_ready[s], it + 2)
                        sp.dma_start(w_raw[s][:], w_qkv[weights]).then_inc(w_in[s], 16)

            def load_half(chunk, half):
                if half == 0:
                    for s in range(SLOTS):
                        sp.wait_ge(tile_stored[s], 16 * ITERS * (chunk + 1))
                if chunk > 0:
                    used = BATCHES * (chunk - 1) + (half + 1) * BATCHES // 2
                    sp.wait_ge(q_packed, used)
                    sp.wait_ge(k_placed, used)
                    sp.wait_ge(v_copied, used)
                for n, dst in enumerate((q_in, k_in, v_in)):
                    for j in range(4):
                        t0 = chunk * CHUNK + j * SUB + half * HALF
                        src = qkv_dram[n * HID:(n + 1) * HID, t0:t0 + HALF].rearrange("(h d) t -> d h t", d=HD)
                        sp.dma_start(dst[32 * j:32 * j + 32, :, half * HALF:(half + 1) * HALF],
                                     src).then_inc(half_in[half], 16)

            def store_o(chunk):
                sp.wait_ge(o_copied, BATCHES * (chunk + 1))
                for j in range(4):
                    t0 = chunk * CHUNK + j * SUB
                    dst = o_dram[:, t0:t0 + SUB].rearrange("(h d) t -> d h t", d=HD)
                    sp.dma_start(dst, o_out[32 * j:32 * j + 32, :, :]).then_inc(o_stored, 16)

            for chunk in range(CHUNKS):
                first = chunk * ITERS
                if chunk == 0:
                    loop(sp, first, ITERS - 2, lambda it: iteration(chunk, it, (it + 2 - first) * SLOTS))
                else:
                    load_half(chunk - 1, 0)
                    iteration(chunk, first, 2 * SLOTS)
                    load_half(chunk - 1, 1)
                    iteration(chunk, first + 1, 3 * SLOTS)
                    if chunk > 1:
                        store_o(chunk - 2)
                    loop(sp, first + 2, ITERS - 4, lambda it: iteration(chunk, it, (it + 2 - first) * SLOTS))
                last = chunk == CHUNKS - 1
                if not last:
                    sp.wait_ge(x_ready, KT * (chunk + 1))
                    sp.dma_start(x_raw[:], x_t[chunk + 1]).then_inc(x_in, 16)
                for n in range(2):
                    iteration(chunk, first + ITERS - 2 + n, None if last else n * SLOTS)
            load_half(CHUNKS - 1, 0)
            load_half(CHUNKS - 1, 1)
            store_o(CHUNKS - 2)
            store_o(CHUNKS - 1)
            sp.wait_ge(o_stored, 64 * CHUNKS)

        @block.gpsimd
        def _(pool):
            nc.gpsimd.memset(k_diag[:], 0.0).then_inc(zeroed, 1)
            nc.gpsimd.memset(v_diag[:], 0.0).then_inc(zeroed, 1)

            def pack(chunk, i, half):
                b = chunk * BATCHES + i
                pool.wait_ge(half_in[half], LOADS_PER_HALF * (chunk + 1))
                t = bass.ds(i * QUADS, QUADS)
                pool.wait_ge(scores_done, b)
                nc.gpsimd.tensor_copy(q_pack[:], q_in[:, :, t].rearrange("p h t -> p t h")).then_inc(q_packed, 1)
                pool.wait_ge(v_packed, b)
                nc.gpsimd.tensor_copy(v_pack[:], v_in[:, :, t].rearrange("p h t -> p t h")).then_inc(v_copied, 1)

            for chunk in range(CHUNKS):
                for half in range(2):
                    loop(pool, half * BATCHES // 2, BATCHES // 2, lambda i: pack(chunk, i, half))

        @block.scalar
        def _(act):
            def split_x(chunk):
                if chunk > 0:
                    act.wait_ge(x_in, 16 * chunk)
                    for s in range(SLOTS):
                        act.wait_ge(tile_done[s], ITERS * chunk)
                for k in range(KT):
                    if chunk == 0:
                        act.wait_ge(x_piece_in[k], 16)
                    nc.scalar.copy(x_hi[:, k, :], x_raw[:, k, :]).then_inc(x_hi_ready, 1)

            def split_w(s, n):
                act.wait_ge(w_in[s], 16 * n + 16)
                act.wait_ge(tile_done[s], n)
                nc.scalar.copy(w_hi[s][:], w_raw[s][:]).then_inc(w_hi_ready[s], 1)

            def place_k(b):
                act.wait_ge(q_packed, b + 1)
                act.wait_ge(scores_done, b)
                t = bass.ds((b % BATCHES) * QUADS, QUADS)
                for j in range(4):
                    g = slice(32 * j, 32 * j + 32)
                    last = nc.scalar.copy(k_diag[g, :, j, :], k_in[g, :, t].rearrange("p h t -> p t h"))
                last.then_inc(k_placed, 1)

            def exponentials(b):
                act.wait_ge(softmax_step, b * SOFTMAX_STEPS + 2)
                nc.scalar.activation(s_exp[:], s_shift[:], ACT.Exp, scale=scale).then_inc(exp_done, 1)

            def copy_probs(b):
                act.wait_ge(probs_turned, b + 1)
                nc.scalar.copy(probs_t[:], probs_ps[:]).then_inc(probs_copied, 1)

            def copy_rows(b):
                act.wait_ge(pv_done, b + 1)
                nc.scalar.copy(o_rows[:], pv_ps[:]).then_inc(pv_copied, 1)

            def copy_o(b):
                act.wait_ge(o_turned, b + 1)
                act.wait_ge(o_stored, (b // BATCHES) * 64)
                t = bass.ds((b % BATCHES) * QUADS, QUADS)
                nc.scalar.copy(o_out[:, :, t].rearrange("p h t -> p t h"), o_ps[:]).then_inc(o_copied, 1)

            def iteration(chunk, it, split, att, before):
                b = it - LAG
                for s in range(SLOTS):
                    if att and s == 0:
                        exponentials(b)
                        place_k(b + 1)
                    act.wait_ge(tile_done[s], it + 1)
                    act.wait_ge(tile_stored[s], 16 * it)
                    m = (it - ITERS * chunk) * SLOTS + s
                    nc.scalar.activation(stage[s][:], tile_ps[s][:], ACT.Identity,
                                         bias=bias[:, bass.ds(m, 1)]).then_inc(tile_staged[s], 1)
                    if split:
                        split_w(s, it + 1)
                    if before and s == 0:
                        copy_o(b - 1)
                    if att and s == 1:
                        copy_probs(b)
                    if att and s == 2:
                        copy_rows(b)

            split_w(0, 0)
            split_x(0)
            for s in range(1, SLOTS):
                split_w(s, 0)
            act.wait_ge(bias_in, 32)
            for first, count, chunk, new_x, split, att in SEGMENTS:
                if new_x and chunk > 0:
                    split_x(chunk)
                if first == LAG:
                    act.wait_ge(zeroed, 2)
                    place_k(0)
                    iteration(chunk, first, split, True, False)
                    first, count = first + 1, count - 1
                loop(act, first, count, lambda it: iteration(chunk, it, split, att, att))

            def tail(b):
                copy_probs(b)
                if not isinstance(b, int) or b < ATT_BATCHES - 1:
                    exponentials(b + 1)
                if not isinstance(b, int):
                    place_k(b + 2)
                copy_rows(b)
                copy_o(b)
            exponentials(TAIL)
            place_k(TAIL + 1)
            copy_o(TAIL - 1)
            loop(act, TAIL, ATT_BATCHES - 2 - TAIL, tail)
            tail(ATT_BATCHES - 2)
            tail(ATT_BATCHES - 1)

        @block.vector
        def _(dve):
            def split_x(chunk):
                for k in range(KT):
                    dve.wait_ge(x_hi_ready, KT * chunk + k + 1)
                    nc.vector.tensor_tensor(x_lo[:, k, :], x_raw[:, k, :], x_hi[:, k, :].bitcast(F32),
                                            ALU.subtract).then_inc(x_ready, 1)

            def split_w(s, n):
                dve.wait_ge(w_hi_ready[s], n + 1)
                nc.vector.tensor_tensor(w_lo[s][:], w_raw[s][:], w_hi[s][:].bitcast(F32),
                                        ALU.subtract).then_inc(w_ready[s], 1)

            def place_v(b):
                dve.wait_ge(v_copied, b + 1)
                dve.wait_ge(pv_done, b)
                for j in range(4):
                    g = slice(32 * j, 32 * j + 32)
                    last = nc.vector.transpose(v_diag[g, :, j, :], v_pack[g, :, :])
                last.then_inc(v_packed, 1)

            def softmax(b):
                step = b * SOFTMAX_STEPS
                dve.wait_ge(scores_done, b + 1)
                nc.vector.tensor_reduce(s_max[:], scores_ps[:], AX.X, ALU.max).then_inc(softmax_step, 1)
                dve.wait_ge(softmax_step, step + 1)
                nc.vector.tensor_tensor(s_shift[:], scores_ps[:],
                                        s_max[:].unsqueeze(2).to_broadcast([P, QUADS, HEADS]),
                                        ALU.subtract).then_inc(softmax_step, 1)
                dve.wait_ge(exp_done, b + 1)
                nc.vector.scalar_tensor_tensor(s_keep[:], scores_ps[:], threshold, s_exp[:],
                                               ALU.is_gt, ALU.mult).then_inc(softmax_step, 1)
                dve.wait_ge(softmax_step, step + 3)
                nc.vector.tensor_reduce(s_sum[:], s_keep[:], AX.X, ALU.add).then_inc(softmax_step, 1)
                dve.wait_ge(softmax_step, step + 4)
                nc.vector.reciprocal(s_inv[:], s_sum[:]).then_inc(softmax_step, 1)
                dve.wait_ge(softmax_step, step + 5)
                nc.vector.tensor_tensor(probs[:], s_keep[:],
                                        s_inv[:].unsqueeze(2).to_broadcast([P, QUADS, HEADS]),
                                        ALU.mult).then_inc(softmax_step, 1)
                place_v(b)

            def iteration(it, split, att):
                if att:
                    softmax(it - LAG)
                if split:
                    for s in range(SLOTS):
                        split_w(s, it + 1)

            split_w(0, 0)
            split_x(0)
            for s in range(1, SLOTS):
                split_w(s, 0)
            for first, count, chunk, new_x, split, att in SEGMENTS:
                if new_x and chunk > 0:
                    split_x(chunk)
                if first == LAG:
                    dve.wait_ge(zeroed, 2)
                loop(dve, first, count, lambda it: iteration(it, split, att))
            loop(dve, TAIL, ATT_BATCHES - TAIL, softmax)

        @block.tensor
        def _(pe):
            def tile(s, new_x, chunk):
                for k in range(KT):
                    if new_x:
                        pe.wait_ge(x_ready, KT * chunk + k + 1)
                    for n, (w, x) in enumerate(((w_hi, x_hi), (w_hi, x_lo), (w_lo, x_hi))):
                        last = nc.tensor.matmul(tile_ps[s][:], w[s][:, k, :], x[:, k, :],
                                                start=(k == 0 and n == 0), stop=(k == KT - 1 and n == 2))
                last.then_inc(tile_done[s], 1)

            def scores(b, read):
                pe.wait_ge(q_packed, b + 1)
                pe.wait_ge(k_placed, b + 1)
                pe.wait_ge(softmax_step, read)
                for t in range(QUADS):
                    u, c = divmod(t, 4)
                    last = nc.tensor.matmul(scores_ps[32 * c:32 * c + 32, 4 * u:4 * u + 4, :], q_pack[:, t, :],
                                            k_diag[:, t, :, :], start=True, stop=True)
                last.then_inc(scores_done, 1)

            def turn_probs(b):
                pe.wait_ge(softmax_step, (b + 1) * SOFTMAX_STEPS)
                pe.wait_ge(probs_copied, b)
                for u in range(4):
                    last = nc.tensor.transpose(probs_ps[:, 4 * u:4 * u + 4, :], probs[:, 4 * u:4 * u + 4, :], ident[:])
                last.then_inc(probs_turned, 1)

            def probs_by_v(b):
                pe.wait_ge(v_packed, b + 1)
                pe.wait_ge(probs_copied, b + 1)
                pe.wait_ge(pv_copied, b)
                for t in range(QUADS):
                    u, c = divmod(t, 4)
                    last = nc.tensor.matmul(pv_ps[32 * c:32 * c + 32, 4 * u:4 * u + 4, :], probs_t[:, t, :],
                                            v_diag[:, t, :, :], start=True, stop=True)
                last.then_inc(pv_done, 1)

            def turn_o(b):
                pe.wait_ge(pv_copied, b + 1)
                pe.wait_ge(o_copied, b)
                for u in range(4):
                    last = nc.tensor.transpose(o_ps[:, 4 * u:4 * u + 4, :], o_rows[:, 4 * u:4 * u + 4, :], ident[:])
                last.then_inc(o_turned, 1)

            def iteration(chunk, it, new_x, att, before):
                b = it - LAG
                if att:
                    scores(b, b * SOFTMAX_STEPS)
                for s in range(SLOTS):
                    pe.wait_ge(w_ready[s], it + 1)
                    pe.wait_ge(tile_staged[s], it)
                    tile(s, new_x and s == 0, chunk)
                    if before and s == 0:
                        turn_o(b - 1)
                    if att and s == 1:
                        turn_probs(b)
                    if att and s == 2:
                        probs_by_v(b)

            for first, count, chunk, new_x, split, att in SEGMENTS:
                if first == LAG:
                    pe.wait_ge(bias_in, 32)
                if new_x or first == LAG:
                    iteration(chunk, first, new_x, att, att and first > LAG)
                    first, count = first + 1, count - 1
                if count:
                    loop(pe, first, count, lambda it: iteration(chunk, it, False, att, att))

            def tail(b):
                scores(b + 1, b * SOFTMAX_STEPS + 3)
                turn_probs(b)
                probs_by_v(b)
                turn_o(b)
            scores(TAIL, TAIL * SOFTMAX_STEPS)
            turn_o(TAIL - 1)
            loop(pe, TAIL, ATT_BATCHES - 1 - TAIL, tail)
            turn_probs(ATT_BATCHES - 1)
            probs_by_v(ATT_BATCHES - 1)
            turn_o(ATT_BATCHES - 1)


SEGMENTS = [
    (0, ITERS, 0, True, True, False),
    (ITERS, LAG - ITERS, 1, True, True, False),
    (LAG, 2 * ITERS - LAG, 1, False, True, True),
    (2 * ITERS, ITERS, 2, True, True, True),
    (3 * ITERS, ITERS - 1, 3, True, True, True),
    (4 * ITERS - 1, 1, 3, False, False, True),
]


def later_stages(nc, sems, o_dram, w_o, b_o, x, identity, identity_bf, w_gu, w_d, x1_dram, x1t_dram, out):
    with ExitStack() as ctx:
        def sb(name, shape, dt=F32, scope=ctx):
            return scope.enter_context(nc.sbuf_tensor(name, shape, dt))

        def sem(name):
            return sems.enter_context(nc.semaphore(name))

        def sem_pair(name):
            return [sem(f"{name}{u}") for u in range(2)]

        ident = sb("ident", [P, P])
        ident_bf = sb("ident_bf", [P, P], BF16)
        raw = [sb(f"raw{u}", [P, PIECE, P]) for u in range(2)]
        slot_hi = [sb(f"slot_hi{u}", [P, PIECE, P], F32R) for u in range(2)]
        slot_lo = [sb(f"slot_lo{u}", [P, PIECE, P], F32R) for u in range(2)]
        silu = sb("silu", [P, FCH])
        val = sb("val", [P, FCH])
        mag = sb("mag", [P, FCH])
        near = sb("near", [P, FCH], BF16)
        sign = sb("sign", [P, FCH], BF16)
        stats = sb("stats", [P, FT, KT, 6])
        moments = sb("moments", [P, FT, 2])
        root = sb("root", [P, FT])
        rstd = sb("rstd", [P, FT])
        shift = sb("shift", [P, FT])
        eps = sb("eps", [P, 1])

        o_raw = [raw[u][:, 0:KT, :] for u in range(2)]
        o_hi = [slot_hi[u][:, 0:KT, :] for u in range(2)]
        o_lo = [slot_lo[u][:, 0:KT, :] for u in range(2)]
        x1t = [buf[:].rearrange("p (k t) -> p k t", t=P) for buf in (val, mag)]
        bo = silu[:]

        half_kt = KT // 2
        with ExitStack() as other_use:
            xt_upper_raw = sb("xt_upper_raw", [P, half_kt, FCH], F32, other_use)
        with ExitStack() as first_use:
            wo_hi = sb("wo_hi", [P, KT, HID], F32R, first_use)
            wo_lo = sb("wo_lo", [P, KT, HID], F32R, first_use)
            x_tok = [sb(f"x_tok{u}", [P, HID], F32, first_use)[:] for u in range(2)]
            y_tok = [sb(f"y_tok{u}", [P, HID], F32, first_use)[:] for u in range(2)]
            x1 = [sb(f"x1_{u}", [P, HID], F32, first_use)[:] for u in range(2)]
        inner = sb("inner", [P, ICH, FCH], F32R)
        with ExitStack() as first_use:
            sb("over_lower_xt_hi", [P, half_kt, FCH], F32, first_use)
            y_first = sb("y_first", [P, half_kt, HID], F32, first_use)
        xt_hi = sb("xt_hi", [P, KT, FCH], F32R)
        with ExitStack() as first_use:
            xt_raw = sb("xt_raw", [P, KT, FCH], F32, first_use)
        xt_lo = sb("xt_lo", [P, KT, FCH], F32R)
        wo_raw = xt_raw
        y = [y_first[:], xt_raw[:, half_kt:KT, :]]

        bank = [ctx.enter_context(nc.psum_tensor(f"bank{n}", [P, FCH], F32)) for n in range(4)]
        proj_ps = [bank[0], bank[1]]
        turn_ps = [bank[2][:].rearrange("p (k t) -> p k t", t=P), bank[3][:].rearrange("p (k t) -> p k t", t=P)]
        gate_ps, up_ps = [bank[0], bank[2]], bank[1]
        down_ps = [[bank[2], bank[3]], [bank[0], bank[3]]]
        quant_ps = [bank[0][:, 0:FCH // 2].bitcast(BF16).rearrange("p (t c) -> p t c", c=P),
                    bank[2][:, 0:FCH // 2].bitcast(BF16).rearrange("p (t c) -> p t c", c=P)]

        consts_in = sem("consts_in")
        eps_set = sem("eps_set")
        wo_in = [sem(f"wo_in{k}") for k in range(KT)]
        wo_hi_ready = sem("wo_hi_ready")
        wo_ready = sem("wo_ready")
        o_in = sem_pair("o_in")
        x_tok_in = sem_pair("x_tok_in")
        o_hi_ready = sem_pair("o_hi_ready")
        o_ready = sem_pair("o_ready")
        proj_done = sem_pair("proj_done")
        biased = sem_pair("biased")
        norm_step = sem_pair("norm_step")
        root1_ready = sem_pair("root1_ready")
        turned1 = sem_pair("turned1")
        turned1_copied = sem_pair("turned1_copied")
        xt_lo_ready = sem_pair("xt_lo_ready")
        x1_stored = sem_pair("x1_stored")
        x1t_stored = sem_pair("x1t_stored")
        w_in = sem_pair("w_in")
        w_hi_ready = sem_pair("w_hi_ready")
        w_ready = sem_pair("w_ready")
        done = [sem("gate_done"), sem("up_done")]
        xt_lower_in = sem("xt_lower_in")
        xt_upper_in = sem("xt_upper_in")
        xt_hi_ready = sem("xt_hi_ready")
        xt_ready = sem("xt_ready")
        silu_ready = sem("silu_ready")
        rest_up_ready = sem("rest_up_ready")
        product = sem("product")
        clipped = sem("clipped")
        mag_ready = sem("mag_ready")
        sign_ready = sem("sign_ready")
        trunc_step = sem("trunc_step")
        rest_copied = sem("rest_copied")
        d_in = sem_pair("d_in")
        d_hi_ready = sem_pair("d_hi_ready")
        d_ready = sem_pair("d_ready")
        d_rest = sem("d_rest")
        piece_done = sem_pair("piece_done")
        y_in = sem("y_in")
        scaled = sem("scaled")
        d_clipped = sem("d_clipped")
        d_sign_ready = sem("d_sign_ready")
        d_mag_ready = sem("d_mag_ready")
        d_step = sem("d_step")
        turned = sem("turned")
        added = sem("added")
        counted = sem("counted")
        moments_ready = sem("moments_ready")
        root_ready = sem("root_ready")
        rstd_ready = sem("rstd_ready")
        normed = [sem("normed_dve"), sem("normed_act")]
        y_stored = [sem(f"y_stored{t}") for t in range(FT)]

        per_u = OUT_TILES // 2

        def gate_slot(chunk, u):
            return (u + chunk) % 2

        def down_slot(chunk, h):
            return (h + 1 + chunk) % 2

        def gate_tile(chunk, u, n):
            return chunk * (ICH if u == 0 else GTILES) + n

        def row_of(buf, n):
            return buf[:, bass.ds(n, 1), :].rearrange("p a t -> p (a t)")

        def xt_src(k):
            upper = isinstance(k, int) and k >= half_kt
            return xt_upper_raw[:, k - half_kt, :] if upper else row_of(xt_raw, k)

        block = ctx.enter_context(nc.Block())

        @block.sync
        def _(sp):
            def load_o(u, t):
                sp.dma_start(o_raw[u], o_dram[:, bass.ds(t, P)].rearrange("(k p) t -> p k t", p=P)
                             ).then_inc(o_in[u], 16)

            def load_w(chunk, u, n, first=False):
                weights = at(sp, n * 2 + u)
                if not first:
                    sp.wait_ge(w_ready[u], gate_tile(chunk, u, n))
                sp.dma_start(raw[u][:, 0:KT, :], w_gu[weights]).then_inc(w_in[u], 16)

            def load_d(chunk, h, j, first=False):
                weights = at(sp, j * 2 + h)
                if not first:
                    sp.wait_ge(d_ready[h], chunk * KT + j)
                sp.dma_start(raw[h][:], w_d[weights]).then_inc(d_in[h], 16)

            def load_xt(dst, k, landed):
                sp.dma_start(dst.rearrange("p (n t) -> p n t", t=P),
                             x1t_dram[:, :, k, :].rearrange("n p t -> p n t")).then_inc(landed, 16)

            load_o(0, 0)
            for k in range(KT):
                sp.dma_start(wo_raw[:, k, :], w_o[k]).then_inc(wo_in[k], 16)
            sp.dma_start(bo, b_o.partition_broadcast(P)).then_inc(consts_in, 16)
            sp.dma_start(x_tok[0], x[0:P, :]).then_inc(x_tok_in[0], 16)
            load_o(1, P)
            sp.dma_start(ident[:], identity).then_inc(consts_in, 16)
            sp.dma_start(ident_bf[:], identity_bf).then_inc(consts_in, 16)
            sp.dma_start(x_tok[1], x[P:2 * P, :]).then_inc(x_tok_in[1], 16)

            def tile(chunk, i, u, load=True):
                if load:
                    t = at(sp, i * (2 * P) + (2 + u) * P)
                    added = at(sp, i * NORM_STEPS + 1)
                    sp.wait_ge(o_ready[u], i + 1)
                    load_o(u, t)
                    sp.wait_ge(norm_step[u], added)
                    sp.dma_start(x_tok[u], x[bass.ds(t, P), :]).then_inc(x_tok_in[u], 16)
                row = at(sp, i * (2 * P) + u * P)
                tile_no = at(sp, i * 2 + u - FT)
                normed_at = at(sp, (i + 1) * NORM_STEPS)
                sp.wait_ge(norm_step[u], normed_at)
                sp.dma_start(x1_dram[bass.ds(row, P), :], x1[u]).then_inc(x1_stored[u], 16)
                if chunk > 0:
                    sp.wait_ge(turned1_copied[u], i + 1)
                    sp.dma_start(x1t_dram[tile_no], x1t[u]).then_inc(x1t_stored[u], 16)

            def both(chunk):
                def run(i):
                    for u in range(2):
                        tile(chunk, i, u)
                return run
            loop(sp, 0, FT // 2, both(0))
            loop(sp, FT // 2, FT // 2 - 1, both(1))
            for u in range(2):
                sp.wait_ge(o_ready[u], per_u)
                load_w(0, u, 0, first=True)
            for u in range(2):
                tile(1, per_u - 1, u, load=False)

            for chunk in range(FCHUNKS):
                last = chunk == FCHUNKS - 1

                def load_pair(n):
                    load_w(chunk, 0, n)
                    load_w(chunk, 1, n)
                if chunk == 0:
                    load_pair(1)
                loop(sp, 2, GTILES - 2, load_pair)
                load_w(chunk, 0, GTILES)
                sp.wait_ge(w_ready[0], gate_tile(chunk, 0, ICH))
                load_d(chunk, 0, 0, first=True)
                sp.wait_ge(w_ready[1], gate_tile(chunk, 1, GTILES))
                load_d(chunk, 1, 0, first=True)
                sp.wait_ge(done[0], gate_tile(chunk, 0, ICH))
                if chunk == 0:
                    for u in range(2):
                        sp.wait_ge(x1_stored[u], 16 * per_u)
                for half in range(2):
                    row = chunk * FCH + half * FCH // 2
                    sp.dma_start(y[half], x1_dram[row:row + FCH // 2, :].rearrange("(t p) c -> p t c", p=P)
                                 ).then_inc(y_in, 16)
                load_d(chunk, 0, 1)
                load_d(chunk, 1, 1)
                if not last:
                    for u in range(2):
                        sp.wait_ge(x1t_stored[u], 16 * FT // 2)
                    for k in range(half_kt):
                        load_xt(xt_raw[:, k, :], k, xt_lower_in)

                def load_pieces(j):
                    load_d(chunk, 0, j)
                    load_d(chunk, 1, j)
                loop(sp, 2, KT - 2, load_pieces)
                if not last:
                    for u in range(2):
                        sp.wait_ge(d_ready[u], (chunk + 1) * KT)
                        load_w(chunk + 1, u, 0, first=True)
                    sp.wait_ge(piece_done[0], (chunk + 1) * KT)
                    for k in range(half_kt, KT):
                        load_xt(xt_upper_raw[:, k - half_kt, :], k, xt_upper_in)
                    load_w(chunk + 1, 0, 1)
                    load_w(chunk + 1, 1, 1)
                for n in range(half_kt):
                    for half in (1, 0):
                        t = half * half_kt + n
                        sp.wait_ge(normed[half], chunk * half_kt + n + 1)
                        row = chunk * FCH + t * P
                        sp.dma_start(out[row:row + P, :], y[half][:, n, :]).then_inc(y_stored[t], 16)
            for t in range(FT):
                sp.wait_ge(y_stored[t], 16 * FCHUNKS)
            for u in range(2):
                sp.wait_ge(x1_stored[u], 16 * per_u)
                sp.wait_ge(x1t_stored[u], 16 * FT // 2)

        @block.gpsimd
        def _(pool):
            pool.wait_ge(consts_in, 48)

            def both(i):
                for u in range(2):
                    pool.wait_ge(x_tok_in[u], 16 * i + 16)
                    nc.gpsimd.tensor_tensor(x_tok[u], x_tok[u], bo, ALU.add).then_inc(biased[u], 1)
            loop(pool, 0, per_u, both)

        @block.scalar
        def _(act):
            def split_o(u, n):
                act.wait_ge(o_in[u], 16 * n + 16)
                act.wait_ge(proj_done[u], n)
                nc.scalar.copy(o_hi[u], o_raw[u]).then_inc(o_hi_ready[u], 1)

            def split_w(chunk, u, n):
                act.wait_ge(w_in[u], gate_tile(chunk, u, n) * 16 + 16)
                if isinstance(n, int) and n == 0:
                    if chunk == 0:
                        act.wait_ge(proj_done[u], per_u)
                    else:
                        act.wait_ge(piece_done[u], chunk * KT)
                else:
                    act.wait_ge(done[u], gate_tile(chunk, u, n))
                nc.scalar.copy(slot_hi[gate_slot(chunk, u)][:, 0:KT, :], raw[u][:, 0:KT, :]).then_inc(w_hi_ready[u], 1)

            def split_d(chunk, h, j):
                act.wait_ge(d_in[h], j * 16 + (chunk * KT + 1) * 16)
                if isinstance(j, int) and j == 0:
                    act.wait_ge(done[1 - h], gate_tile(chunk, 1 - h, ICH if h == 1 else GTILES))
                else:
                    act.wait_ge(piece_done[h], chunk * KT + j)
                nc.scalar.copy(slot_hi[down_slot(chunk, h)][:], raw[h][:]).then_inc(d_hi_ready[h], 1)

            def split_xt(k):
                nc.scalar.copy(row_of(xt_hi, k), xt_src(k)).then_inc(xt_hi_ready, 1)

            act.wait_ge(o_in[0], 16)
            split_o(0, 0)
            for k in range(KT):
                act.wait_ge(wo_in[k], 16)
                nc.scalar.copy(wo_hi[:, k, :], wo_raw[:, k, :]).then_inc(wo_hi_ready, 1)
            split_o(1, 0)
            act.wait_ge(eps_set, 1)

            def take_root(i, u):
                act.wait_ge(norm_step[u], i * NORM_STEPS + 5)
                nc.scalar.activation(root[:, u:u + 1], moments[:, u, 1:2], ACT.Sqrt, bias=eps[:]
                                     ).then_inc(root1_ready[u], 1)

            def take_turned(chunk, i, u):
                act.wait_ge(turned1[u], i + 1)
                if chunk == 0:
                    nc.scalar.copy(xt_hi[:, :, bass.ds(i * (2 * P) + u * P, P)], turn_ps[u]
                                   ).then_inc(turned1_copied[u], 1)
                else:
                    act.wait_ge(x1t_stored[u], i * 16 - 16 * FT // 2)
                    nc.scalar.copy(x1t[u], turn_ps[u]).then_inc(turned1_copied[u], 1)

            def both(chunk):
                def run(i):
                    for u in range(2):
                        split_o(u, i + 1)
                        take_root(i, u)
                        take_turned(chunk, i, u)
                return run
            loop(act, 0, FT // 2, both(0))
            loop(act, FT // 2, FT // 2 - 1, both(1))
            take_root(per_u - 1, 0)
            split_w(0, 0, 0)
            take_turned(1, per_u - 1, 0)
            take_root(per_u - 1, 1)
            split_w(0, 1, 0)
            take_turned(1, per_u - 1, 1)
            act.wait_ge(biased[1], per_u)
            for u in range(2):
                act.wait_ge(x1t_stored[u], 16 * FT // 2)

            for chunk in range(FCHUNKS):
                def tile(n, rows, next_up):
                    count = chunk * ICH + n
                    act.wait_ge(done[0], count + 1)
                    act.wait_ge(product, count)
                    nc.scalar.activation(silu[0:rows, :], gate_ps[chunk][0:rows, :], ACT.Silu,
                                         scale=1.0 / 128.0).then_inc(silu_ready, 1)
                    if rows < P:
                        act.wait_ge(trunc_step, count * TRUNC_STEPS)
                        nc.scalar.copy(mag[0:rows, :], gate_ps[chunk][rows:2 * rows, :]).then_inc(rest_up_ready, 1)
                    else:
                        split_w(chunk, 0, n + 1)
                    if next_up:
                        split_w(chunk, 1, n + 1)
                    else:
                        split_d(chunk, 0 if rows == P else 1, 0)
                    act.wait_ge(clipped, count + 1)
                    nc.scalar.activation(mag[0:rows, :], val[0:rows, :], ACT.Abs).then_inc(mag_ready, 1)
                    nc.scalar.activation(sign[0:rows, :], val[0:rows, :], ACT.Sign, scale=-1.0
                                         ).then_inc(sign_ready, 1)

                loop(act, 0, GTILES - 1, lambda n: tile(n, P, True))
                tile(GTILES - 1, P, False)
                tile(GTILES, REST, False)
                act.wait_ge(trunc_step, (chunk + 1) * ICH * TRUNC_STEPS)
                nc.scalar.copy(inner[REST:2 * REST, GTILES, :], inner[0:REST, GTILES, :].bitcast(F32)
                               ).then_inc(rest_copied, 1)

                def quantise(j, u):
                    count = chunk * KT + j
                    for h in range(2):
                        act.wait_ge(piece_done[h], count + 1)
                    act.wait_ge(d_step, count * TRUNC_STEPS)
                    act.wait_ge(d_sign_ready, count)
                    nc.scalar.mul(val[:], down_ps[chunk][u][:], 128.0).then_inc(scaled, 1)
                    act.wait_ge(d_clipped, count + 1)
                    nc.scalar.activation(mag[:], val[:], ACT.Abs).then_inc(d_mag_ready, 1)
                    nc.scalar.activation(sign[:], val[:], ACT.Sign, scale=-1.0).then_inc(d_sign_ready, 1)

                xt_piece = chunk < FCHUNKS - 1
                split_d(chunk, 0, 1)

                def pair_d(i, xt):
                    for u in range(2):
                        j = i * 2 + u
                        split_d(chunk, 1, j + 1)
                        quantise(j, u)
                        split_d(chunk, 0, j + 2)
                        if xt:
                            split_xt(j)
                if xt_piece:
                    act.wait_ge(xt_lower_in, 16 * half_kt)
                    loop(act, 0, half_kt // 2, lambda i: pair_d(i, True))
                    pair_d(half_kt // 2, False)
                else:
                    loop(act, 0, KT // 2 - 1, lambda i: pair_d(i, False))
                split_d(chunk, 1, KT - 1)
                quantise(KT - 2, 0)
                if xt_piece:
                    split_w(chunk + 1, 0, 0)
                    split_w(chunk + 1, 1, 0)
                quantise(KT - 1, 1)
                act.wait_ge(moments_ready, (chunk + 1) * FT)
                nc.scalar.activation(root[:], moments[:, :, 1], ACT.Sqrt, bias=eps[:]).then_inc(root_ready, 1)
                act.wait_ge(rstd_ready, 2 * (chunk + 1))
                for n in range(half_kt):
                    t = half_kt + n
                    nc.scalar.activation(y[1][:, n, :], y[1][:, n, :], ACT.Identity, bias=shift[:, t:t + 1],
                                         scale=rstd[:, t:t + 1]).then_inc(normed[1], 1)
                if xt_piece:
                    act.wait_ge(xt_upper_in, 16 * half_kt)
                    for n in range(half_kt):
                        act.wait_ge(y_stored[n], 16)
                        split_xt(half_kt + n)

        @block.vector
        def _(dve):
            def low(dst, src, hi):
                return nc.vector.tensor_tensor(dst, src, hi.bitcast(F32), ALU.subtract)

            def split_o(u, n):
                dve.wait_ge(o_hi_ready[u], n + 1)
                low(o_lo[u], o_raw[u], o_hi[u]).then_inc(o_ready[u], 1)

            def split_w(chunk, u, n):
                s = gate_slot(chunk, u)
                dve.wait_ge(w_hi_ready[u], gate_tile(chunk, u, n) + 1)
                low(slot_lo[s][:, 0:KT, :], raw[u][:, 0:KT, :], slot_hi[s][:, 0:KT, :]).then_inc(w_ready[u], 1)

            def split_d(chunk, h, j):
                s = down_slot(chunk, h)
                dve.wait_ge(d_hi_ready[h], j + (chunk * KT + 1))
                if h == 0:
                    low(slot_lo[s][:], raw[h][:], slot_hi[s][:]).then_inc(d_ready[h], 1)
                else:
                    rest = slice(REST, 2 * REST)
                    low(slot_lo[s][:, 0:PIECE - 1, :], raw[h][:, 0:PIECE - 1, :], slot_hi[s][:, 0:PIECE - 1, :]
                        ).then_inc(d_rest, 1)
                    low(slot_hi[s][rest, PIECE - 1, :], raw[h][rest, PIECE - 1, :], slot_hi[s][rest, PIECE - 1, :]
                        ).then_inc(d_ready[h], 1)

            def split_xt(k):
                low(row_of(xt_lo, k), xt_src(k), row_of(xt_hi, k)).then_inc(xt_ready, 1)

            nc.vector.memset(eps[:], EPS).then_inc(eps_set, 1)
            split_o(0, 0)
            for k in range(KT):
                dve.wait_ge(wo_hi_ready, k + 1)
                low(wo_lo[:, k, :], wo_raw[:, k, :], wo_hi[:, k, :]).then_inc(wo_ready, 1)
            split_o(1, 0)

            def tile(i, u, split):
                step = i * NORM_STEPS
                dve.wait_ge(proj_done[u], i + 1)
                dve.wait_ge(biased[u], i + 1)
                nc.vector.tensor_tensor(y_tok[u], proj_ps[u][:], x_tok[u], ALU.add).then_inc(norm_step[u], 1)
                dve.wait_ge(norm_step[u], step + 1)
                for n in range(2):
                    nc.vector.bn_stats(stats[:, u, n, :], y_tok[u][:, n * 512:(n + 1) * 512]).then_inc(norm_step[u], 1)
                if split:
                    split_o(u, i + 1)
                dve.wait_ge(norm_step[u], step + 3)
                nc.vector.bn_aggr(moments[:, u, :], stats[:, u, 0:2, :]).then_inc(norm_step[u], 2)
                dve.wait_ge(root1_ready[u], i + 1)
                nc.vector.reciprocal(rstd[:, u:u + 1], root[:, u:u + 1]).then_inc(norm_step[u], 1)
                dve.wait_ge(norm_step[u], step + 6)
                dve.wait_ge(x1_stored[u], 16 * i)
                dve.wait_ge(turned1[u], i)
                nc.vector.tensor_scalar(x1[u], y_tok[u], moments[:, u, 0:1], rstd[:, u:u + 1],
                                        ALU.subtract, ALU.mult).then_inc(norm_step[u], 1)

            def low_turned(i, u):
                dve.wait_ge(turned1_copied[u], i + 1)
                t = bass.ds(i * (2 * P) + u * P, P)
                low(xt_lo[:, :, t], turn_ps[u], xt_hi[:, :, t]).then_inc(xt_lo_ready[u], 1)

            tile(0, 0, True)
            tile(0, 1, True)
            low_turned(0, 0)

            def both(i):
                tile(i, 0, True)
                low_turned(i - 1, 1)
                tile(i, 1, True)
                low_turned(i, 0)
            loop(dve, 1, FT // 2 - 1, both)
            tile(FT // 2, 0, True)
            low_turned(FT // 2 - 1, 1)
            tile(FT // 2, 1, True)

            def both_later(i):
                tile(i, 0, True)
                tile(i, 1, True)
            loop(dve, FT // 2 + 1, FT // 2 - 2, both_later)
            tile(per_u - 1, 0, False)
            split_w(0, 0, 0)
            tile(per_u - 1, 1, False)
            split_w(0, 1, 0)
            for u in range(2):
                dve.wait_ge(x1t_stored[u], 16 * FT // 2)
                dve.wait_ge(x1_stored[u], 16 * per_u)

            for chunk in range(FCHUNKS):
                def tile_g(n, rows, next_up):
                    r = slice(0, rows)
                    count = chunk * ICH + n
                    step = count * TRUNC_STEPS
                    if rows == P:
                        split_w(chunk, 0, n + 1)
                    dve.wait_ge(silu_ready, count + 1)
                    dve.wait_ge(sign_ready, count)
                    if rows == P:
                        dve.wait_ge(done[1], gate_tile(chunk, 1, n) + 1)
                        nc.vector.tensor_tensor(val[r, :], up_ps[r, :], silu[r, :], ALU.mult).then_inc(product, 1)
                    else:
                        dve.wait_ge(rest_up_ready, chunk + 1)
                        nc.vector.tensor_tensor(val[r, :], mag[r, :], silu[r, :], ALU.mult).then_inc(product, 1)
                    dve.wait_ge(product, count + 1)
                    nc.vector.tensor_scalar(val[r, :], val[r, :], -128.0, 127.0, ALU.max, ALU.min).then_inc(clipped, 1)
                    if next_up:
                        split_w(chunk, 1, n + 1)
                    else:
                        split_d(chunk, 0 if rows == P else 1, 0)
                    dve.wait_ge(mag_ready, count + 1)
                    nc.vector.tensor_scalar(near[r, :], mag[r, :], ROUND, ROUND, ALU.add, ALU.subtract
                                            ).then_inc(trunc_step, 1)
                    dve.wait_ge(trunc_step, step + 1)
                    nc.vector.tensor_tensor(mag[r, :], near[r, :], mag[r, :], ALU.is_gt).then_inc(trunc_step, 1)
                    dve.wait_ge(trunc_step, step + 2)
                    nc.vector.tensor_tensor(near[r, :], mag[r, :], near[r, :], ALU.subtract).then_inc(trunc_step, 1)
                    dve.wait_ge(trunc_step, step + 3)
                    dve.wait_ge(sign_ready, count + 1)
                    nc.vector.tensor_tensor(inner[r, bass.ds(n, 1), :].rearrange("p a t -> p (a t)"), near[r, :],
                                            sign[r, :], ALU.mult).then_inc(trunc_step, 2)

                loop(dve, 0, GTILES - 1, lambda n: tile_g(n, P, True))
                tile_g(GTILES - 1, P, False)
                tile_g(GTILES, REST, False)

                def clip(j):
                    dve.wait_ge(scaled, chunk * KT + j + 1)
                    nc.vector.tensor_scalar(val[:], val[:], -128.0, 127.0, ALU.max, ALU.min).then_inc(d_clipped, 1)

                def truncate(j):
                    count = chunk * KT + j
                    step = count * TRUNC_STEPS
                    dve.wait_ge(d_mag_ready, count + 1)
                    dve.wait_ge(turned, count)
                    nc.vector.tensor_scalar(near[:], mag[:], ROUND, ROUND, ALU.add, ALU.subtract).then_inc(d_step, 1)
                    dve.wait_ge(d_step, step + 1)
                    nc.vector.tensor_tensor(mag[:], near[:], mag[:], ALU.is_gt).then_inc(d_step, 1)
                    dve.wait_ge(d_step, step + 2)
                    nc.vector.tensor_tensor(near[:], mag[:], near[:], ALU.subtract).then_inc(d_step, 1)
                    dve.wait_ge(d_step, step + 3)
                    dve.wait_ge(d_sign_ready, count + 1)
                    nc.vector.tensor_tensor(near[:], near[:], sign[:], ALU.mult).then_inc(d_step, 2)

                def add(j):
                    dve.wait_ge(turned, chunk * KT + j + 1)
                    c = bass.ds(j * P, P)
                    for half in range(2):
                        tiles = slice(half * half_kt, (half + 1) * half_kt)
                        nc.vector.tensor_tensor(y[half][:, :, c], quant_ps[chunk][:, tiles, :], y[half][:, :, c],
                                                ALU.add).then_inc(added, 1)

                def count_in(j):
                    dve.wait_ge(added, (chunk * KT + j) * 2 + 2)
                    c = bass.ds(j * P, P)
                    for t in range(FT):
                        last = nc.vector.bn_stats(stats[:, t, bass.ds(j, 1), :].rearrange("p a s -> p (a s)"),
                                                  y[t // half_kt][:, t % half_kt, c])
                    last.then_inc(counted, 1)

                xt_piece = chunk < FCHUNKS - 1

                def take_xt(k):
                    dve.wait_ge(xt_hi_ready, k + 1)
                    split_xt(k)

                split_d(chunk, 0, 1)
                split_d(chunk, 1, 1)
                clip(0)
                truncate(0)
                split_d(chunk, 0, 2)
                dve.wait_ge(y_in, 32 * (chunk + 1))

                def step_d(j, xt=False):
                    if xt:
                        take_xt(j - 2)
                    split_d(chunk, 1, j)
                    add(j - 2)
                    clip(j - 1)
                    count_in(j - 2)
                    truncate(j - 1)
                    split_d(chunk, 0, j + 1)
                if xt_piece:
                    loop(dve, 2, half_kt, lambda j: step_d(j, xt=True))
                    step_d(KT - 2)
                else:
                    loop(dve, 2, KT - 3, step_d)
                split_d(chunk, 1, KT - 1)
                add(KT - 3)
                clip(KT - 2)
                count_in(KT - 3)
                truncate(KT - 2)
                if xt_piece:
                    split_w(chunk + 1, 0, 0)
                    split_w(chunk + 1, 1, 0)
                clip(KT - 1)
                add(KT - 2)
                truncate(KT - 1)
                count_in(KT - 2)
                add(KT - 1)
                count_in(KT - 1)
                dve.wait_ge(counted, (chunk + 1) * KT)
                for t in range(FT):
                    nc.vector.bn_aggr(moments[:, t, :], stats[:, t, :, :]).then_inc(moments_ready, 1)
                dve.wait_ge(root_ready, chunk + 1)
                nc.vector.reciprocal(rstd[:], root[:]).then_inc(rstd_ready, 1)
                dve.wait_ge(rstd_ready, 2 * chunk + 1)
                nc.vector.scalar_tensor_tensor(shift[:], moments[:, :, 0], -1.0, rstd[:], ALU.mult, ALU.mult
                                               ).then_inc(rstd_ready, 1)
                for t in range(half_kt):
                    nc.vector.tensor_scalar(y[0][:, t, :], y[0][:, t, :], moments[:, t, 0:1], rstd[:, t:t + 1],
                                            ALU.subtract, ALU.mult).then_inc(normed[0], 1)
                if xt_piece:
                    for k in range(half_kt, KT):
                        dve.wait_ge(y_stored[k], 16)
                        take_xt(k)

        @block.tensor
        def _(pe):
            def project(i, u, first=False):
                pe.wait_ge(o_ready[u], i + 1)
                pe.wait_ge(norm_step[u], i * NORM_STEPS)
                for k in range(KT):
                    if first:
                        pe.wait_ge(wo_ready, k + 1)
                    for m, (o, w) in enumerate(((o_hi, wo_hi), (o_hi, wo_lo), (o_lo, wo_hi))):
                        for n in range(2):
                            last = nc.tensor.matmul(proj_ps[u][:, n * 512:(n + 1) * 512], o[u][:, k, :],
                                                    w[:, k, n * 512:(n + 1) * 512],
                                                    start=(k == 0 and m == 0), stop=(k == KT - 1 and m == 2))
                last.then_inc(proj_done[u], 1)

            def turn_x1(chunk, i, u):
                pe.wait_ge(norm_step[u], (i + 1) * NORM_STEPS)
                pe.wait_ge(turned1_copied[u], i)
                if chunk == 0:
                    pe.wait_ge(xt_lo_ready[u], i)
                else:
                    pe.wait_ge(xt_lo_ready[u], FT // 2)
                for k in range(KT):
                    last = nc.tensor.transpose(turn_ps[u][:, k, :], x1[u][:, k * P:(k + 1) * P], ident[:])
                last.then_inc(turned1[u], 1)

            project(0, 0, first=True)
            pe.wait_ge(consts_in, 48)

            def both(chunk):
                def run(i):
                    project(i, 1)
                    turn_x1(chunk, i, 0)
                    project(i + 1, 0)
                    turn_x1(chunk, i, 1)
                return run
            loop(pe, 0, FT // 2, both(0))
            loop(pe, FT // 2, FT // 2 - 1, both(1))
            project(per_u - 1, 1)
            turn_x1(1, per_u - 1, 0)

            def products(chunk, u, ks):
                s = gate_slot(chunk, u)
                ps = up_ps if u else gate_ps[chunk]
                for k in ks:
                    for m, (w, xt) in enumerate(((slot_hi, xt_hi), (slot_hi, xt_lo), (slot_lo, xt_hi))):
                        for h in range(2):
                            last = nc.tensor.matmul(ps[:, h * 512:(h + 1) * 512], w[s][:, k, :],
                                                    xt[:, k, h * 512:(h + 1) * 512],
                                                    start=(k == 0 and m == 0), stop=(k == KT - 1 and m == 2))
                return last

            def tile_g(chunk, u, n):
                pe.wait_ge(w_ready[u], gate_tile(chunk, u, n) + 1)
                pe.wait_ge(product if u else silu_ready, chunk * ICH + n)
                products(chunk, u, range(KT)).then_inc(done[u], 1)

            def piece(chunk, j, u, h):
                s = down_slot(chunk, h)
                pe.wait_ge(d_ready[h], j + (chunk * KT + 1))
                for c in range(PIECE):
                    rest = h == 1 and c == PIECE - 1
                    for m, w in enumerate((slot_hi,) if rest else (slot_hi, slot_lo)):
                        for half in range(2):
                            last = nc.tensor.matmul(down_ps[chunk][u][:, half * 512:(half + 1) * 512], w[s][:, c, :],
                                                    inner[:, h * PIECE + c, half * 512:(half + 1) * 512],
                                                    start=(h == 0 and c == 0 and m == 0), stop=rest)
                last.then_inc(piece_done[h], 1)

            def turn_quant(chunk, j):
                count = chunk * KT + j
                pe.wait_ge(d_step, count * TRUNC_STEPS + TRUNC_STEPS)
                pe.wait_ge(added, count * 2)
                for t in range(FT):
                    last = nc.tensor.transpose(quant_ps[chunk][:, t, :], near[:, t * P:(t + 1) * P], ident_bf[:])
                last.then_inc(turned, 1)

            for u in range(2):
                pe.wait_ge(xt_lo_ready[u], FT // 2)
                pe.wait_ge(norm_step[u], (per_u - 1) * NORM_STEPS + 1)
                if u == 0:
                    tile_g(0, 0, 0)
                    turn_x1(1, per_u - 1, 1)
                else:
                    tile_g(0, 1, 0)

            for chunk in range(FCHUNKS):
                last_chunk = chunk == FCHUNKS - 1

                def pair_g(n):
                    tile_g(chunk, 0, n)
                    tile_g(chunk, 1, n)
                loop(pe, 1, GTILES - 1, pair_g)
                pe.wait_ge(silu_ready, chunk * ICH + GTILES)
                tile_g(chunk, 0, GTILES)

                pe.wait_ge(added, chunk * KT * 2)
                pe.wait_ge(trunc_step, (chunk * ICH + PIECE) * TRUNC_STEPS)
                piece(chunk, 0, 0, 0)
                pe.wait_ge(rest_copied, chunk + 1)
                piece(chunk, 0, 0, 1)
                pe.wait_ge(scaled, chunk * KT)
                piece(chunk, 1, 1, 0)
                piece(chunk, 1, 1, 1)
                turn_quant(chunk, 0)

                def pair_d(i):
                    for u in range(2):
                        j = i * 2 + u
                        pe.wait_ge(scaled, j - 1 + chunk * KT)
                        piece(chunk, j, u, 0)
                        piece(chunk, j, u, 1)
                        turn_quant(chunk, j - 1)
                loop(pe, 1, KT // 2 - 1, pair_d)
                if not last_chunk:
                    nxt = chunk + 1
                    pe.wait_ge(xt_ready, half_kt)
                    pe.wait_ge(scaled, chunk * KT + KT - 1)
                    pe.wait_ge(w_ready[0], gate_tile(nxt, 0, 0) + 1)
                    products(nxt, 0, range(half_kt))
                    pe.wait_ge(w_ready[1], gate_tile(nxt, 1, 0) + 1)
                    products(nxt, 1, (0,))
                turn_quant(chunk, KT - 1)
                if not last_chunk:
                    products(nxt, 1, range(1, half_kt))
                    for u, k in ((0, 4), (1, 4), (0, 5), (1, 5), (0, 6), (0, 7), (1, 6), (1, 7)):
                        pe.wait_ge(xt_ready, k + 1)
                        last = products(nxt, u, (k,))
                        if k == KT - 1:
                            last.then_inc(done[u], 1)


def build(nc, ins, out):
    qkv_dram = nc.dram_tensor("qkv_scratch", (3 * HID, TOKENS), F32).ap()
    o_dram = nc.dram_tensor("o_scratch", (HID, TOKENS), F32).ap()
    x1_dram = nc.dram_tensor("x1_scratch", (TOKENS, HID), F32).ap()
    x1t_dram = nc.dram_tensor("x1t_scratch", (FT, P, KT, P), F32).ap()
    with ExitStack() as sems:
        attention_stage(nc, sems, ins["x_t"], ins["w_qkv"], ins["b_qkv"], ins["identity"], qkv_dram, o_dram)
        later_stages(nc, sems, o_dram, ins["w_o"], ins["b_o"], ins["x"], ins["identity"], ins["identity_bf"],
                     ins["w_gu"], ins["w_d"], x1_dram, x1t_dram, out)


def kernel(L0_attn_x, L0_attn_Wq, L0_attn_bq, L0_attn_Wk, L0_attn_bk, L0_attn_Wv, L0_attn_bv, L0_attn_Wo,
           L0_attn_bo, L0_ffn_w_gate, L0_ffn_w_up, L0_ffn_w_down):
    import ml_dtypes
    import concourse.bacc as bacc
    from concourse.bass_utils import run_bass_kernel_spmd

    shape = L0_attn_x.shape
    x = np.ascontiguousarray(L0_attn_x).reshape(TOKENS, HID)

    def tiles(w):
        return np.asarray(w).reshape(-1, P, KT, P).transpose(0, 3, 2, 1)

    gate, up = np.asarray(L0_ffn_w_gate), np.asarray(L0_ffn_w_up)
    whole = GTILES * P
    pairs = np.stack([tiles(gate[:whole]), tiles(up[:whole])], axis=1).reshape(2 * GTILES, P, KT, P)
    rest = tiles(np.concatenate([gate[whole:], up[whole:]]))
    wd = np.asarray(L0_ffn_w_down)
    wd = np.concatenate([wd, wd[:, whole:]], axis=1).reshape(KT, P, 2, PIECE, P).transpose(0, 2, 4, 3, 1)
    wd = wd.reshape(2 * KT, P, PIECE, P)
    arrays = {
        "x": x,
        "x_t": x.reshape(CHUNKS, CHUNK, KT, P).transpose(0, 3, 2, 1),
        "w_qkv": tiles(np.concatenate([L0_attn_Wq, L0_attn_Wk, L0_attn_Wv])),
        "b_qkv": np.concatenate([L0_attn_bq, L0_attn_bk, L0_attn_bv]).reshape(QKV_TILES, P).T,
        "w_o": np.asarray(L0_attn_Wo).T.reshape(KT, P, HID),
        "b_o": np.asarray(L0_attn_bo),
        "identity": np.eye(P, dtype=np.float32),
        "identity_bf": np.eye(P, dtype=ml_dtypes.bfloat16),
        "w_gu": np.concatenate([pairs, rest]),
        "w_d": wd,
    }
    nc = bacc.Bacc("TRN2", target_bir_lowering=False, num_devices=1)
    arrays = {n: np.ascontiguousarray(a) for n, a in arrays.items()}
    ins = {n: nc.dram_tensor(f"in_{n}", a.shape, mybir.dt.from_np(a.dtype), kind="ExternalInput").ap()
           for n, a in arrays.items()}
    out = nc.dram_tensor("out", (TOKENS, HID), F32, kind="ExternalOutput").ap()
    build(nc, ins, out)
    run = run_bass_kernel_spmd(nc, [{f"in_{n}": a for n, a in arrays.items()}], core_ids=[0])
    return run.results[0]["out"].reshape(shape)
```

```python
from contextlib import ExitStack

import numpy as np

import concourse.bass as bass
from concourse import mybir
from concourse.alu_op_type import AluOpType as ALU

F32 = mybir.dt.float32
F32R = mybir.dt.float32r
BF16 = mybir.dt.bfloat16
ACT = mybir.ActivationFunctionType
AX = mybir.AxisListType

P = 128
TOKENS = 2048
HID = 1024
KT = HID // P
HEADS = 32
HD = HID // HEADS
INTER = 2752
EPS = 1e-5

CHUNK = 512
CHUNKS = TOKENS // CHUNK
SUB = CHUNK // 4
SLOTS = 3
QKV_TILES = 3 * HID // P
ITERS = QKV_TILES // SLOTS
QUADS = 16
BATCHES = SUB // QUADS
HALF = SUB // 2
LAG = ITERS + 2
QKV_ITERS = CHUNKS * ITERS
ATT_BATCHES = CHUNKS * BATCHES
TAIL = QKV_ITERS - LAG
LOADS_PER_HALF = 3 * 4 * 16
SOFTMAX_STEPS = 6
NORM_STEPS = 7
TRUNC_STEPS = 5

FCH = 1024
FCHUNKS = TOKENS // FCH
FT = FCH // P
GTILES = INTER // P
REST = INTER - GTILES * P
ICH = GTILES + 1
PIECE = ICH // 2
ROUND = 1.5 * 2.0**23
OUT_TILES = TOKENS // P
WHOLE = KT - 1


def score_scale():
    return np.float32(1.0 / np.sqrt(HD))


def raw_threshold():
    scale, limit = score_scale(), np.float32(0.001)
    s = np.float32(limit / scale)
    while np.float32(s * scale) > limit:
        s = np.nextafter(s, np.float32(0), dtype=np.float32)
    while np.float32(np.nextafter(s, np.float32(1), dtype=np.float32) * scale) <= limit:
        s = np.nextafter(s, np.float32(1), dtype=np.float32)
    return float(s)


def loop(eng, first, count, body, peel=None):
    for _ in range(int(first == 0) if peel is None else peel):
        body(first)
        first, count = first + 1, count - 1
    if count == 1:
        body(first)
    elif count:
        with eng.Fori(first, first + count) as i:
            body(i)


def at(eng, value):
    return value if isinstance(value, int) else eng.snap(value)


def memory(nc, ctx):
    m = {}
    half_kt = KT // 2

    def sb(scope, name, shape, dt=F32):
        m[name] = scope.enter_context(nc.sbuf_tensor(name, shape, dt))

    def ps(scope, name, shape):
        m[name] = scope.enter_context(nc.psum_tensor(name, shape, F32))

    with ExitStack() as stage1:
        sb(stage1, "x_raw", [P, KT, CHUNK])
        sb(stage1, "x_hi", [P, KT, CHUNK], F32R)
        sb(stage1, "x_lo", [P, KT, CHUNK], F32R)
        for s in range(SLOTS):
            sb(stage1, f"w_raw{s}", [P, KT, P])
            sb(stage1, f"w_hi{s}", [P, KT, P], F32R)
            sb(stage1, f"w_lo{s}", [P, KT, P], F32R)
    with ExitStack() as stage2:
        sb(stage2, "wo_hi", [P, KT, HID], F32R)
        with ExitStack() as unsplit:
            sb(unsplit, "wo_raw", [P, KT, HID])
        sb(stage2, "wo_lo", [P, KT, HID], F32R)
        for u in range(2):
            sb(stage2, f"x_tok{u}", [P, HID])
            sb(stage2, f"y_tok{u}", [P, HID])
            sb(stage2, f"x1_{u}", [P, HID])
    with ExitStack() as second_chunk:
        sb(second_chunk, "xt_upper_raw", [P, half_kt, FCH])
    sb(ctx, "inner", [P, ICH, FCH], F32R)

    sb(ctx, "ident", [P, P])
    sb(ctx, "ident_bf", [P, P], BF16)
    sb(ctx, "stats", [P, FT, KT, 6])
    sb(ctx, "moments", [P, FT, 2])
    for name in ("root", "rstd", "shift"):
        sb(ctx, name, [P, FT])
    sb(ctx, "eps", [P, 1])

    with ExitStack() as stage1:
        for s in range(SLOTS):
            sb(stage1, f"stage{s}", [P, CHUNK])
    with ExitStack() as beside_attention:
        sb(beside_attention, "bo", [P, HID])
        for u in range(2):
            sb(beside_attention, f"first_o_hi{u}", [P, KT, P], F32R)
            sb(beside_attention, f"first_o_lo{u}", [P, KT, P], F32R)
        after = 2 * 2 * KT * P * 4 + HID * 4 - (3 * FCH * 4 + 2 * FCH * 2)
    for name in ("silu", "val", "mag"):
        sb(ctx, name, [P, FCH])
    for name in ("near", "sign"):
        sb(ctx, name, [P, FCH], BF16)
    sb(ctx, "gap", [P, after // 4])

    with ExitStack() as attention:
        for name in ("q_in", "k_in", "v_in"):
            sb(attention, name, [P, 2, HEADS, HALF])
        sb(attention, "k_diag", [P, QUADS, 4, HEADS])
        sb(attention, "v_diag", [P, QUADS, 4, HD])
        for name in ("q_pack", "v_pack", "s_shift", "s_exp", "s_keep", "probs", "probs_t", "o_rows"):
            sb(attention, name, [P, QUADS, HEADS])
        for name in ("s_max", "s_sum", "s_inv"):
            sb(attention, name, [P, QUADS])
        sb(attention, "bias", [P, QKV_TILES])
        sb(attention, "o_out", [P, HEADS, SUB])
    for u in range(2):
        sb(ctx, f"raw{u}", [P, PIECE, P])
    for u in range(2):
        sb(ctx, f"slot_hi{u}", [P, PIECE, P], F32R)
        sb(ctx, f"slot_lo{u}", [P, PIECE, P], F32R)
    with ExitStack() as residual:
        sb(residual, "over_lower_xt_hi", [P, half_kt, FCH])
        sb(residual, "y_first", [P, half_kt, HID])
    sb(ctx, "xt_hi", [P, KT, FCH], F32R)
    with ExitStack() as unsplit:
        sb(unsplit, "xt_raw", [P, KT, FCH])
    sb(ctx, "xt_lo", [P, KT, FCH], F32R)

    with ExitStack() as stage1:
        for s in range(SLOTS):
            ps(stage1, f"tile_ps{s}", [P, CHUNK])
        ps(stage1, "unused", [P, CHUNK])
        ps(stage1, "scores_ps", [P, QUADS, HEADS])
        ps(stage1, "pv_ps", [P, QUADS, HD])
        ps(stage1, "probs_ps", [P, QUADS, HEADS])
        ps(stage1, "o_ps", [P, QUADS, HEADS])
    with ExitStack() as beside_attention:
        ps(beside_attention, "proj_ps", [P, HID])
        ps(beside_attention, "turn_ps", [P, KT, P])
    for n in range(4):
        ps(ctx, f"bank{n}", [P, FCH])
    return m


def attention_programs(nc, sems, m, hand, start, x_t, w_qkv, b_qkv, identity, identity_bf,
                       qkv_dram, o_dram, w_o, b_o, x,
                       x1_dram, x1t_dram):
    scale, threshold = float(score_scale()), raw_threshold()

    def sem(name):
        return sems.enter_context(nc.semaphore(name))

    def trio(name):
        return [m[f"{name}{s}"] for s in range(SLOTS)]

    def pair_of(name):
        return [m[f"{name}{u}"] for u in range(2)]

    x_raw, x_hi, x_lo, bias, ident, ident_bf = (
        m[n] for n in ("x_raw", "x_hi", "x_lo", "bias", "ident", "ident_bf"))
    w_raw, w_hi, w_lo, tile_ps = (trio(n) for n in ("w_raw", "w_hi", "w_lo", "tile_ps"))
    stage = [buf[:] for buf in trio("stage")]
    q_in, k_in, v_in, k_diag, v_diag, q_pack, v_pack = (
        m[n] for n in ("q_in", "k_in", "v_in", "k_diag", "v_diag", "q_pack", "v_pack"))
    s_shift, s_exp, s_keep, probs, probs_t, o_rows, s_max, s_sum, s_inv, o_out = (
        m[n] for n in ("s_shift", "s_exp", "s_keep", "probs", "probs_t", "o_rows", "s_max", "s_sum", "s_inv", "o_out"))
    scores_ps, pv_ps, probs_ps, o_ps = (m[n] for n in ("scores_ps", "pv_ps", "probs_ps", "o_ps"))
    wo_raw, wo_hi, wo_lo, bo, proj_ps, turn_ps, eps = (
        m[n] for n in ("wo_raw", "wo_hi", "wo_lo", "bo", "proj_ps", "turn_ps", "eps"))
    o_hi, o_lo, x_tok, y_tok = (pair_of(n) for n in ("first_o_hi", "first_o_lo", "x_tok", "y_tok"))
    o_raw = [buf[:].rearrange("p (k t) -> p k t", t=P) for buf in pair_of("x1_")]
    x1t = [buf[:].rearrange("p (k t) -> p k t", t=P) for buf in x_tok]
    stats, moments, root, rstd = m["stats"][:, 0, 0:2, :], m["moments"][:, 0, :], m["root"][:, 0:1], m["rstd"][:, 0:1]

    q_packed, k_placed, v_copied, o_copied, o_stored, norm_step, x1_turned, x1t_copied, x1_stored, x1t_stored = (
        hand[n] for n in ("q_packed", "k_placed", "v_copied", "o_copied", "o_stored", "first_norm_step", "x1_turned",
                          "x1t_copied", "first_x1_stored", "first_x1t_stored"))
    bias_in = sem("bias_in")
    x_in = sem("x_in")
    x_piece_in = [sem(f"x_piece_in{k}") for k in range(KT)]
    x_hi_ready = sem("x_hi_ready")
    x_ready = sem("x_ready")
    w_in = [sem(f"qkv_w_in{s}") for s in range(SLOTS)]
    w_hi_ready = [sem(f"qkv_w_hi_ready{s}") for s in range(SLOTS)]
    w_ready = [sem(f"qkv_w_ready{s}") for s in range(SLOTS)]
    tile_done = [sem(f"tile_done{s}") for s in range(SLOTS)]
    tile_staged = [sem(f"tile_staged{s}") for s in range(SLOTS)]
    tile_stored = [sem(f"tile_stored{s}") for s in range(SLOTS)]
    half_in = [sem(f"half_in{h}") for h in range(2)]
    zeroed = sem("zeroed")
    v_packed = sem("v_packed")
    scores_done = sem("scores_done")
    softmax_step = sem("softmax_step")
    exp_done = sem("exp_done")
    probs_turned = sem("probs_turned")
    probs_copied = sem("probs_copied")
    pv_done = sem("pv_done")
    pv_copied = sem("pv_copied")
    o_turned = sem("o_turned")
    wo_in = [sem(f"wo_in{k}") for k in range(KT)]
    wo_hi_ready = sem("wo_hi_ready")
    wo_ready = sem("wo_ready")
    bo_in = sem("bo_in")
    eps_set = sem("first_eps_set")
    o_in = [sem(f"first_o_in{u}") for u in range(2)]
    o_hi_ready = sem("first_o_hi_ready")
    o_ready = sem("first_o_ready")
    x_tok_in = [sem(f"first_x_tok_in{u}") for u in range(2)]
    biased = sem("first_biased")
    proj_done = sem("first_proj_done")
    root_ready = sem("first_root_ready")

    def tail(eng, step):
        def pair(i, last=False):
            step(i * 2, 0, False)
            step(i * 2 + 1, 1, last)
        loop(eng, 0, FT // 2 - 1, pair)
        pair(FT // 2 - 1, last=True)

    def sync(sp):
        sp.dma_start(w_raw[0][:], w_qkv[0]).then_inc(w_in[0], 16)
        for k in range(KT):
            sp.dma_start(x_raw[:, k, :], x_t[0, :, k, :]).then_inc(x_piece_in[k], 16)
        for s in range(1, SLOTS):
            sp.dma_start(w_raw[s][:], w_qkv[s]).then_inc(w_in[s], 16)
        sp.dma_start(bias[:], b_qkv).then_inc(bias_in, 16)
        sp.dma_start(ident[:], identity).then_inc(bias_in, 16)
        sp.dma_start(ident_bf[:], identity_bf).then_inc(bias_in, 16)
        for s in range(SLOTS):
            sp.wait_ge(w_ready[s], 1)
            sp.dma_start(w_raw[s][:], w_qkv[SLOTS + s]).then_inc(w_in[s], 16)

        def iteration(chunk, it, load_tile):
            for s in range(SLOTS):
                row = at(sp, (it - ITERS * chunk) * (SLOTS * P) + s * P)
                tile = qkv_dram[chunk, :, bass.ds(row, P), :].rearrange("b p t -> p b t")
                weights = None if load_tile is None else at(sp, load_tile + s)
                sp.wait_ge(tile_staged[s], it + 1)
                sp.dma_start(tile, stage[s].rearrange("p (b t) -> p b t", t=HALF)
                             ).then_inc(tile_stored[s], 16)
                if load_tile is not None:
                    sp.wait_ge(w_ready[s], it + 2)
                    sp.dma_start(w_raw[s][:], w_qkv[weights]).then_inc(w_in[s], 16)

        def load_half(chunk, half):
            if half == 0:
                for s in range(SLOTS):
                    sp.wait_ge(tile_stored[s], 16 * ITERS * (chunk + 1))
            if chunk > 0:
                used = BATCHES * (chunk - 1) + (half + 1) * BATCHES // 2
                sp.wait_ge(q_packed, used)
                sp.wait_ge(k_placed, used)
                sp.wait_ge(v_copied, used)
            for n, dst in enumerate((q_in, k_in, v_in)):
                for j in range(4):
                    src = qkv_dram[chunk, 2 * j + half, n * HID:(n + 1) * HID, :]
                    sp.dma_start(dst[32 * j:32 * j + 32, half, :, :],
                                 src.rearrange("(d h) t -> d h t", d=HD)).then_inc(half_in[half], 16)

        def store_o(chunk):
            sp.wait_ge(o_copied, BATCHES * (chunk + 1))
            for j in range(4):
                t0 = chunk * CHUNK + j * SUB
                dst = o_dram[:, t0:t0 + SUB].rearrange("(h d) t -> d h t", d=HD)
                sp.dma_start(dst, o_out[32 * j:32 * j + 32, :, :]).then_inc(o_stored, 16)

        for chunk in range(CHUNKS):
            first = chunk * ITERS
            if chunk == 0:
                loop(sp, first, ITERS - 2, lambda it: iteration(chunk, it, (it + 2 - first) * SLOTS))
            else:
                load_half(chunk - 1, 0)
                iteration(chunk, first, 2 * SLOTS)
                load_half(chunk - 1, 1)
                iteration(chunk, first + 1, 3 * SLOTS)
                if chunk > 1:
                    store_o(chunk - 2)
                loop(sp, first + 2, ITERS - 4, lambda it: iteration(chunk, it, (it + 2 - first) * SLOTS))
            last = chunk == CHUNKS - 1
            if not last:
                sp.wait_ge(x_ready, KT * (chunk + 1))
                sp.dma_start(x_raw[:], x_t[chunk + 1]).then_inc(x_in, 16)
            for n in range(2):
                iteration(chunk, first + ITERS - 2 + n, None if last else n * SLOTS)
        for s in range(SLOTS):
            sp.wait_ge(tile_done[s], QKV_ITERS)
            sp.wait_ge(w_ready[s], QKV_ITERS)

        def load_o(t, u):
            cols = at(sp, t * P)
            if not isinstance(t, int) or t > 1:
                sp.wait_ge(o_ready, t - 1)
            sp.dma_start(o_raw[u], o_dram[:, bass.ds(cols, P)].rearrange("(k p) t -> p k t", p=P)
                         ).then_inc(o_in[u], 16)

        load_o(0, 0)
        for k in range(KT):
            sp.dma_start(wo_raw[:, k, :], w_o[k]).then_inc(wo_in[k], 16)
        load_half(CHUNKS - 1, 0)
        load_o(1, 1)
        sp.dma_start(bo[:], b_o.partition_broadcast(P)).then_inc(bo_in, 16)
        for u in range(2):
            sp.dma_start(x_tok[u][:], x[u * P:(u + 1) * P, :]).then_inc(x_tok_in[u], 16)
        load_half(CHUNKS - 1, 1)

        def finish_tile(t, u, more):
            row = at(sp, t * P)
            next_row = at(sp, t * P + 2 * P)
            tile_no = at(sp, t + 0)
            normed_at = at(sp, (t + 1) * NORM_STEPS)
            stored_at = at(sp, (t // 2) * 16 + 16) if isinstance(t, int) else at(sp, (t + 2 - u) * 8)
            if more:
                load_o(t + 2, u)
            sp.wait_ge(norm_step, normed_at)
            sp.dma_start(x1_dram[bass.ds(row, P), :], y_tok[u][:]).then_inc(x1_stored[u], 16)
            sp.wait_ge(x1t_copied, t + 1)
            sp.dma_start(x1t_dram[tile_no], x1t[u]).then_inc(x1t_stored[u], 16)
            if more:
                sp.wait_ge(x1t_stored[u], stored_at)
                sp.dma_start(x_tok[u][:], x[bass.ds(next_row, P), :]).then_inc(x_tok_in[u], 16)

        def pair(i):
            for u in range(2):
                finish_tile(i * 2 + u, u, True)
        finish_tile(0, 0, True)
        store_o(CHUNKS - 2)
        finish_tile(1, 1, True)
        loop(sp, 1, FT // 2 - 2, pair)
        sp.wait_ge(q_packed, ATT_BATCHES)
        sp.wait_ge(o_stored, 64 * (CHUNKS - 1))
        for u in range(2):
            start["load_o"](sp, u)
        for u in range(2):
            finish_tile(FT - 2 + u, u, False)
            sp.wait_ge(x1t_stored[u], 16 * FT // 2)
            start["load_x"](sp, u)
            start["load_next_o"](sp, 0, u)
        store_o(CHUNKS - 1)

    def gpsimd(pool):
        nc.gpsimd.memset(k_diag[:], 0.0).then_inc(zeroed, 1)
        nc.gpsimd.memset(v_diag[:], 0.0).then_inc(zeroed, 1)

        def pack(chunk, i, half, between=None):
            b = chunk * BATCHES + i
            pool.wait_ge(half_in[half], LOADS_PER_HALF * (chunk + 1))
            t = bass.ds((i - half * (BATCHES // 2)) * QUADS, QUADS)
            pool.wait_ge(scores_done, b)
            nc.gpsimd.tensor_copy(q_pack[:], q_in[:, half, :, t].rearrange("p h t -> p t h")).then_inc(q_packed, 1)
            if between:
                between()
            pool.wait_ge(v_packed, b)
            nc.gpsimd.tensor_copy(v_pack[:], v_in[:, half, :, t].rearrange("p h t -> p t h")).then_inc(v_copied, 1)

        for chunk in range(CHUNKS - 1):
            for half in range(2):
                loop(pool, half * BATCHES // 2, BATCHES // 2, lambda i: pack(chunk, i, half))

        def add_bias(t, u):
            if isinstance(t, int) and t == 0:
                pool.wait_ge(bo_in, 16)
            pool.wait_ge(x_tok_in[u], (t - u) * 8 + 16)
            nc.gpsimd.tensor_tensor(x_tok[u][:], x_tok[u][:], bo[:], ALU.add).then_inc(biased, 1)

        for half in range(2):
            def pair(i):
                for u in range(2):
                    pack(CHUNKS - 1, i * 2 + u, half, between=lambda: add_bias(i * 2 + u, u))
            loop(pool, half * BATCHES // 4, BATCHES // 4, pair)

    def scalar(act):
        def split_x(chunk):
            if chunk > 0:
                act.wait_ge(x_in, 16 * chunk)
                for s in range(SLOTS):
                    act.wait_ge(tile_done[s], ITERS * chunk)
            for k in range(KT):
                if chunk == 0:
                    act.wait_ge(x_piece_in[k], 16)
                nc.scalar.copy(x_hi[:, k, :], x_raw[:, k, :]).then_inc(x_hi_ready, 1)

        def split_w(s, n):
            act.wait_ge(w_in[s], 16 * n + 16)
            act.wait_ge(tile_done[s], n)
            nc.scalar.copy(w_hi[s][:], w_raw[s][:]).then_inc(w_hi_ready[s], 1)

        def place_k(b):
            act.wait_ge(q_packed, b + 1)
            act.wait_ge(scores_done, b)
            half = bass.ds(b // (BATCHES // 2) % 2, 1)
            t = bass.ds((b % (BATCHES // 2)) * QUADS, QUADS)
            for j in range(4):
                g = slice(32 * j, 32 * j + 32)
                last = nc.scalar.copy(k_diag[g, :, j, :], k_in[g, half, :, t].rearrange("p a h t -> p t (a h)"))
            last.then_inc(k_placed, 1)

        def exponentials(b):
            act.wait_ge(softmax_step, b * SOFTMAX_STEPS + 2)
            nc.scalar.activation(s_exp[:], s_shift[:], ACT.Exp, scale=scale).then_inc(exp_done, 1)

        def copy_probs(b):
            act.wait_ge(probs_turned, b + 1)
            nc.scalar.copy(probs_t[:], probs_ps[:]).then_inc(probs_copied, 1)

        def copy_rows(b):
            act.wait_ge(pv_done, b + 1)
            nc.scalar.copy(o_rows[:], pv_ps[:]).then_inc(pv_copied, 1)

        def copy_o(b, first_chunk=False):
            act.wait_ge(o_turned, b + 1)
            if not first_chunk:
                act.wait_ge(o_stored, (b // BATCHES) * 64)
            t = bass.ds((b % BATCHES) * QUADS, QUADS)
            nc.scalar.copy(o_out[:, :, t].rearrange("p h t -> p t h"), o_ps[:]).then_inc(o_copied, 1)

        def iteration(chunk, it, split, att, before, o_used, x_changes=False):
            b = it - LAG
            for s in range(SLOTS):
                if att and s == 0:
                    exponentials(b)
                    place_k(b + 1)
                if x_changes and s == SLOTS - 1:
                    split_x(chunk + 1)
                act.wait_ge(tile_done[s], it + 1)
                act.wait_ge(tile_stored[s], 16 * it)
                m = (it - ITERS * chunk) * SLOTS + s
                nc.scalar.activation(stage[s], tile_ps[s][:], ACT.Identity,
                                     bias=bias[:, bass.ds(m, 1)]).then_inc(tile_staged[s], 1)
                if split:
                    split_w(s, it + 1)
                if before and s == 0:
                    copy_o(b - 1, not o_used)
                if att and s == 1:
                    copy_probs(b)
                if att and s == 2:
                    copy_rows(b)

        split_w(0, 0)
        split_x(0)
        for s in range(1, SLOTS):
            split_w(s, 0)
        act.wait_ge(bias_in, 48)
        for first, count, chunk, new_x, next_x, split, att in SEGMENTS:
            if first == ITERS:
                loop(act, first, count - 1, lambda it: iteration(chunk, it, split, False, False, False))
                first, count = first + count - 1, 1
                act.wait_ge(zeroed, 2)
                place_k(0)
            if first == LAG:
                iteration(chunk, first, split, True, False, False)
                first, count = first + 1, count - 1
            o_used = first > LAG + BATCHES
            loop(act, first, count, lambda it: iteration(chunk, it, split, att, att, o_used, next_x))

        def split_wo(k):
            act.wait_ge(wo_in[k], 16)
            nc.scalar.copy(wo_hi[:, k, :], wo_raw[:, k, :]).then_inc(wo_hi_ready, 1)

        def split_o(t, u):
            act.wait_ge(o_in[u], (t - u) * 8 + 16)
            if not isinstance(t, int) or t > 1:
                act.wait_ge(proj_done, t - 1)
            nc.scalar.copy(o_hi[u][:], o_raw[u]).then_inc(o_hi_ready, 1)

        def take_x1t(t, u):
            act.wait_ge(x1_turned, t + 1)
            nc.scalar.copy(x1t[u], turn_ps[:]).then_inc(x1t_copied, 1)

        def batch(b, next_k=True):
            exponentials(b)
            if next_k:
                place_k(b + 1)

        batch(TAIL)
        copy_o(TAIL - 1)
        copy_probs(TAIL)
        copy_rows(TAIL)
        split_o(0, 0)
        for k in range(KT):
            split_wo(k)
        act.wait_ge(eps_set, 1)

        def step(t, u, last):
            b = t + (TAIL + 1)
            batch(b)
            if not last:
                split_o(t + 1, 1 - u)
            copy_o(b - 1)
            if not isinstance(t, int) or t > 0:
                take_x1t(t - 1, 1 - u)
            copy_probs(b)
            if last:
                start["split_hi"](act, 0)
            copy_rows(b)
            act.wait_ge(norm_step, t * NORM_STEPS + 5)
            nc.scalar.activation(root[:], moments[:, 1:2], ACT.Sqrt, bias=eps[:]).then_inc(root_ready, 1)
        tail(act, step)
        b = ATT_BATCHES - 1
        batch(b, next_k=False)
        start["split_hi"](act, 1)
        copy_o(b - 1)
        take_x1t(FT - 1, 1)
        copy_probs(b)
        copy_rows(b)
        copy_o(b)

    def vector(dve):
        def split_x(chunk):
            for k in range(KT):
                dve.wait_ge(x_hi_ready, KT * chunk + k + 1)
                nc.vector.tensor_tensor(x_lo[:, k, :], x_raw[:, k, :], x_hi[:, k, :].bitcast(F32),
                                        ALU.subtract).then_inc(x_ready, 1)

        def split_w(s, n):
            dve.wait_ge(w_hi_ready[s], n + 1)
            nc.vector.tensor_tensor(w_lo[s][:], w_raw[s][:], w_hi[s][:].bitcast(F32),
                                    ALU.subtract).then_inc(w_ready[s], 1)

        def place_v(b):
            dve.wait_ge(v_copied, b + 1)
            dve.wait_ge(pv_done, b)
            for j in range(4):
                g = slice(32 * j, 32 * j + 32)
                last = nc.vector.transpose(v_diag[g, :, j, :], v_pack[g, :, :])
            last.then_inc(v_packed, 1)

        def softmax(b):
            step = b * SOFTMAX_STEPS
            dve.wait_ge(scores_done, b + 1)
            nc.vector.tensor_reduce(s_max[:], scores_ps[:], AX.X, ALU.max).then_inc(softmax_step, 1)
            dve.wait_ge(softmax_step, step + 1)
            nc.vector.tensor_tensor(s_shift[:], scores_ps[:],
                                    s_max[:].unsqueeze(2).to_broadcast([P, QUADS, HEADS]),
                                    ALU.subtract).then_inc(softmax_step, 1)
            dve.wait_ge(exp_done, b + 1)
            nc.vector.scalar_tensor_tensor(s_keep[:], scores_ps[:], threshold, s_exp[:],
                                           ALU.is_gt, ALU.mult).then_inc(softmax_step, 1)
            dve.wait_ge(softmax_step, step + 3)
            nc.vector.tensor_reduce(s_sum[:], s_keep[:], AX.X, ALU.add).then_inc(softmax_step, 1)
            dve.wait_ge(softmax_step, step + 4)
            nc.vector.reciprocal(s_inv[:], s_sum[:]).then_inc(softmax_step, 1)
            dve.wait_ge(softmax_step, step + 5)
            nc.vector.tensor_tensor(probs[:], s_keep[:],
                                    s_inv[:].unsqueeze(2).to_broadcast([P, QUADS, HEADS]),
                                    ALU.mult).then_inc(softmax_step, 1)
            place_v(b)

        def iteration(chunk, it, split, att, x_changes):
            if att:
                softmax(it - LAG)
            if split:
                for s in range(SLOTS):
                    if x_changes and s == SLOTS - 1:
                        split_x(chunk + 1)
                    split_w(s, it + 1)

        split_w(0, 0)
        split_x(0)
        for s in range(1, SLOTS):
            split_w(s, 0)
        for first, count, chunk, new_x, next_x, split, att in SEGMENTS:
            if first == LAG:
                dve.wait_ge(zeroed, 2)
            loop(dve, first, count, lambda it: iteration(chunk, it, split, att, next_x), peel=int(first in (0, LAG)))

        nc.vector.memset(eps[:], EPS).then_inc(eps_set, 1)
        softmax(TAIL)

        def split_o(t, u):
            dve.wait_ge(o_hi_ready, t + 1)
            nc.vector.tensor_tensor(o_lo[u][:], o_raw[u], o_hi[u][:].bitcast(F32),
                                    ALU.subtract).then_inc(o_ready, 1)

        def norm(t, u):
            at_step = t * NORM_STEPS
            dve.wait_ge(proj_done, t + 1)
            dve.wait_ge(biased, t + 1)
            if not isinstance(t, int) or t > 1:
                dve.wait_ge(x1_stored[u], (t - u) * 8)
                dve.wait_ge(x1_turned, t - 1)
            nc.vector.tensor_tensor(y_tok[u][:], proj_ps[:], x_tok[u][:], ALU.add).then_inc(norm_step, 1)
            dve.wait_ge(norm_step, at_step + 1)
            for n in range(2):
                nc.vector.bn_stats(stats[:, n, :], y_tok[u][:, n * 512:(n + 1) * 512]).then_inc(norm_step, 1)
            dve.wait_ge(norm_step, at_step + 3)
            nc.vector.bn_aggr(moments[:], stats[:]).then_inc(norm_step, 2)
            dve.wait_ge(root_ready, t + 1)
            nc.vector.reciprocal(rstd[:], root[:]).then_inc(norm_step, 1)
            dve.wait_ge(norm_step, at_step + 6)
            nc.vector.tensor_scalar(y_tok[u][:], y_tok[u][:], moments[:, 0:1], rstd[:],
                                    ALU.subtract, ALU.mult).then_inc(norm_step, 1)

        split_o(0, 0)
        for k in range(KT):
            dve.wait_ge(wo_hi_ready, k + 1)
            nc.vector.tensor_tensor(wo_lo[:, k, :], wo_raw[:, k, :], wo_hi[:, k, :].bitcast(F32),
                                    ALU.subtract).then_inc(wo_ready, 1)

        def step(t, u, last):
            softmax(t + (TAIL + 1))
            if last:
                start["split_lo"](dve, 0)
            else:
                split_o(t + 1, 1 - u)
            norm(t, u)
        tail(dve, step)
        softmax(ATT_BATCHES - 1)

    def tensor(pe):
        def tile(s, new_x, chunk):
            for k in range(KT):
                if new_x:
                    pe.wait_ge(x_ready, KT * chunk + k + 1)
                for n, (w, x) in enumerate(((w_hi, x_hi), (w_hi, x_lo), (w_lo, x_hi))):
                    last = nc.tensor.matmul(tile_ps[s][:], w[s][:, k, :], x[:, k, :],
                                            start=(k == 0 and n == 0), stop=(k == KT - 1 and n == 2))
            last.then_inc(tile_done[s], 1)

        def scores(b, read):
            pe.wait_ge(q_packed, b + 1)
            pe.wait_ge(k_placed, b + 1)
            pe.wait_ge(softmax_step, read)
            for t in range(QUADS):
                u, c = divmod(t, 4)
                last = nc.tensor.matmul(scores_ps[32 * c:32 * c + 32, 4 * u:4 * u + 4, :], q_pack[:, t, :],
                                        k_diag[:, t, :, :], start=True, stop=True)
            last.then_inc(scores_done, 1)

        def turn_probs(b):
            pe.wait_ge(softmax_step, (b + 1) * SOFTMAX_STEPS)
            pe.wait_ge(probs_copied, b)
            for u in range(4):
                last = nc.tensor.transpose(probs_ps[:, 4 * u:4 * u + 4, :], probs[:, 4 * u:4 * u + 4, :], ident[:])
            last.then_inc(probs_turned, 1)

        def probs_by_v(b):
            pe.wait_ge(v_packed, b + 1)
            pe.wait_ge(probs_copied, b + 1)
            pe.wait_ge(pv_copied, b)
            for t in range(QUADS):
                u, c = divmod(t, 4)
                last = nc.tensor.matmul(pv_ps[32 * c:32 * c + 32, 4 * u:4 * u + 4, :], probs_t[:, t, :],
                                        v_diag[:, t, :, :], start=True, stop=True)
            last.then_inc(pv_done, 1)

        def turn_o(b):
            pe.wait_ge(pv_copied, b + 1)
            pe.wait_ge(o_copied, b)
            for u in range(4):
                last = nc.tensor.transpose(o_ps[:, 4 * u:4 * u + 4, :], o_rows[:, 4 * u:4 * u + 4, :], ident[:])
            last.then_inc(o_turned, 1)

        def iteration(chunk, it, new_x, att, before):
            b = it - LAG
            if att:
                scores(b, b * SOFTMAX_STEPS)
            for s in range(SLOTS):
                pe.wait_ge(w_ready[s], it + 1)
                pe.wait_ge(tile_staged[s], it)
                tile(s, new_x and s == 0, chunk)
                if before and s == 0:
                    turn_o(b - 1)
                if att and s == 1:
                    turn_probs(b)
                if att and s == 2:
                    probs_by_v(b)

        for first, count, chunk, new_x, next_x, split, att in SEGMENTS:
            if first == LAG:
                pe.wait_ge(bias_in, 48)
            if new_x or first == LAG:
                iteration(chunk, first, new_x, att, att and first > LAG)
                first, count = first + 1, count - 1
            loop(pe, first, count, lambda it: iteration(chunk, it, False, att, att),
                 peel=int(first == LAG + 1))

        scores(TAIL, TAIL * SOFTMAX_STEPS)
        turn_o(TAIL - 1)
        turn_probs(TAIL)
        probs_by_v(TAIL)
        for s in range(SLOTS):
            pe.wait_ge(tile_staged[s], QKV_ITERS)

        def project(t, u, ks, first):
            for k in ks:
                if first:
                    pe.wait_ge(wo_ready, k + 1)
                for m, (o, w) in enumerate(((o_hi, wo_hi), (o_hi, wo_lo), (o_lo, wo_hi))):
                    for n in range(2):
                        last = nc.tensor.matmul(proj_ps[:, n * 512:(n + 1) * 512], o[u][:, k, :],
                                                w[:, k, n * 512:(n + 1) * 512],
                                                start=(k == 0 and m == 0), stop=(k == KT - 1 and m == 2))
            return last

        def turn_x1(t, u):
            pe.wait_ge(norm_step, (t + 1) * NORM_STEPS)
            if not isinstance(t, int) or t > 0:
                pe.wait_ge(x1t_copied, t)
            for k in range(KT):
                last = nc.tensor.transpose(turn_ps[:, k, :], y_tok[u][:, k * P:(k + 1) * P], ident[:])
            last.then_inc(x1_turned, 1)

        def step(t, u, last):
            b = t + (TAIL + 1)
            first = isinstance(t, int) and t == 0
            scores(b, b * SOFTMAX_STEPS)
            pe.wait_ge(o_ready, t + 1)
            if not first:
                pe.wait_ge(norm_step, (t - 1) * NORM_STEPS + 1)
            project(t, u, range(0, 3), first)
            turn_o(b - 1)
            if not first:
                turn_x1(t - 1, 1 - u)
            project(t, u, range(3, 6), first)
            turn_probs(b)
            project(t, u, range(6, KT), first).then_inc(proj_done, 1)
            probs_by_v(b)
        tail(pe, step)
        b = ATT_BATCHES - 1
        scores(b, b * SOFTMAX_STEPS)
        start["project"](pe)
        turn_o(b - 1)
        turn_x1(FT - 1, 1)
        turn_probs(b)
        probs_by_v(b)
        turn_o(b)

    return {"sync": sync, "gpsimd": gpsimd, "scalar": scalar, "vector": vector, "tensor": tensor}


SEGMENTS = [
    (0, ITERS - 1, 0, True, False, True, False),
    (ITERS - 1, 1, 0, False, True, True, False),
    (ITERS, LAG - ITERS, 1, True, False, True, False),
    (LAG, 2 * ITERS - 1 - LAG, 1, False, False, True, True),
    (2 * ITERS - 1, 1, 1, False, True, True, True),
    (2 * ITERS, LAG + 1 - ITERS, 2, True, False, True, True),
    (LAG + BATCHES + 1, 2 * ITERS - LAG - 2, 2, False, False, True, True),
    (3 * ITERS - 1, 1, 2, False, True, True, True),
    (3 * ITERS, ITERS - 1, 3, True, False, True, True),
    (4 * ITERS - 1, 1, 3, False, False, False, True),
]


def later_programs(nc, sems, m, hand, o_dram, x, w_gu, w_d, x1_dram, x1t_dram, out):
    def sem(name):
        return sems.enter_context(nc.semaphore(name))

    def sem_pair(name):
        return [sem(f"{name}{u}") for u in range(2)]

    def pair_of(name):
        return [m[f"{name}{u}"] for u in range(2)]

    half_kt = KT // 2
    inner, wo_hi, wo_lo, xt_hi, xt_lo, xt_raw, xt_upper_raw = (
        m[n] for n in ("inner", "wo_hi", "wo_lo", "xt_hi", "xt_lo", "xt_raw", "xt_upper_raw"))
    silu, val, mag, near, sign, stats, moments, root, rstd, shift, eps, ident, ident_bf = (
        m[n] for n in ("silu", "val", "mag", "near", "sign", "stats", "moments", "root", "rstd", "shift", "eps",
                       "ident", "ident_bf"))
    raw, slot_hi, slot_lo = (pair_of(n) for n in ("raw", "slot_hi", "slot_lo"))
    x_tok, y_tok, x1 = ([buf[:] for buf in pair_of(n)] for n in ("x_tok", "y_tok", "x1_"))
    bo = m["bo"][:]
    o_raw, o_hi, o_lo = ([buf[:, 0:KT, :] for buf in pair_of(n)] for n in ("raw", "slot_hi", "slot_lo"))
    x1t = [buf[:].rearrange("p (k t) -> p k t", t=P) for buf in (val, mag)]
    y = [m["y_first"][:], xt_raw[:, half_kt:KT, :]]

    bank = [m[f"bank{n}"] for n in range(4)]
    proj_ps = [bank[0], bank[1]]
    turn_ps = [bank[2][:].rearrange("p (k t) -> p k t", t=P), bank[3][:].rearrange("p (k t) -> p k t", t=P)]
    gate_ps, up_ps = [bank[0], bank[2]], bank[1]
    down_ps = [[bank[2], bank[3]], [bank[0], bank[3]]]
    quant_ps = [bank[0][:, 0:FCH // 2].bitcast(BF16).rearrange("p (t c) -> p t c", c=P),
                bank[2][:, 0:FCH // 2].bitcast(BF16).rearrange("p (t c) -> p t c", c=P)]

    o_in = sem_pair("o_in")
    x_tok_in = sem_pair("x_tok_in")
    o_hi_ready = sem_pair("o_hi_ready")
    o_ready = sem_pair("o_ready")
    proj_done = sem_pair("proj_done")
    biased = sem_pair("biased")
    norm_step = sem_pair("norm_step")
    root1_ready = sem_pair("root1_ready")
    turned1 = sem_pair("turned1")
    turned1_copied = sem_pair("turned1_copied")
    xt_first_in = sem_pair("xt_first_in")
    x1_stored = sem_pair("x1_stored")
    x1t_stored = sem_pair("x1t_stored")
    w_in = sem_pair("w_in")
    w_hi_ready = sem_pair("w_hi_ready")
    w_ready = sem_pair("w_ready")
    done = [sem("gate_done"), sem("up_done")]
    xt_lower_in = sem("xt_lower_in")
    xt_upper_in = sem("xt_upper_in")
    xt_hi_ready = sem("xt_hi_ready")
    xt_ready = sem("xt_ready")
    silu_ready = sem("silu_ready")
    rest_up_ready = sem("rest_up_ready")
    product = sem("product")
    clipped = sem("clipped")
    mag_ready = sem("mag_ready")
    sign_ready = sem("sign_ready")
    trunc_step = sem("trunc_step")
    rest_copied = sem("rest_copied")
    d_in = sem_pair("d_in")
    d_hi_ready = sem_pair("d_hi_ready")
    d_ready = sem_pair("d_ready")
    d_rest = sem("d_rest")
    piece_done = sem_pair("piece_done")
    y_in = sem("y_in")
    d_sign_ready = sem("d_sign_ready")
    d_mag_ready = sem("d_mag_ready")
    d_step = sem("d_step")
    turned = sem("turned")
    added = sem("added")
    counted = sem("counted")
    moments_ready = sem("moments_ready")
    root_ready = sem("root_ready")
    rstd_ready = sem("rstd_ready")
    normed = [sem("normed_dve"), sem("normed_act")]
    first_half_done = sem("first_half_done")
    half_mag_ready = sem("half_mag_ready")
    half_sign_ready = sem("half_sign_ready")
    half_step = sem("half_step")
    half_turned = sem("half_turned")
    half_added = sem("half_added")
    half_counted = sem("half_counted")
    y_stored = [sem(f"y_stored{t}") for t in range(FT)]

    per_u = FT // 2

    def gate_slot(chunk, u):
        return (u + chunk) % 2

    def down_slot(chunk, h):
        return (h + 1 + chunk) % 2

    def gate_tile(chunk, u, n):
        return chunk * (ICH if u == 0 else GTILES) + n

    def row_of(buf, n):
        return buf[:, bass.ds(n, 1), :].rearrange("p a t -> p (a t)")

    def xt_src(k, upper):
        return xt_upper_raw[:, k - half_kt, :] if upper else row_of(xt_raw, k)

    def load_o(sp, u):
        sp.dma_start(o_raw[u], o_dram[:, FCH + u * P:FCH + (u + 1) * P].rearrange("(k p) t -> p k t", p=P)
                     ).then_inc(o_in[u], 16)

    def load_next_o(sp, i, u):
        cols = FCH + (2 * i + u + 2) * P
        sp.wait_ge(o_ready[u], i + 1)
        sp.dma_start(o_raw[u], o_dram[:, cols:cols + P].rearrange("(k p) t -> p k t", p=P)).then_inc(o_in[u], 16)

    def load_x(sp, u):
        sp.dma_start(x_tok[u], x[FCH + u * P:FCH + (u + 1) * P, :]).then_inc(x_tok_in[u], 16)

    def split_hi(act, u):
        for taken in ("q_packed", "k_placed", "v_copied"):
            act.wait_ge(hand[taken], ATT_BATCHES)
        act.wait_ge(o_in[u], 16)
        nc.scalar.copy(o_hi[u], o_raw[u]).then_inc(o_hi_ready[u], 1)

    def split_lo(dve, u):
        dve.wait_ge(o_hi_ready[u], 1)
        nc.vector.tensor_tensor(o_lo[u], o_raw[u], o_hi[u].bitcast(F32), ALU.subtract).then_inc(o_ready[u], 1)

    def project(pe, i, u):
        pe.wait_ge(o_ready[u], i + 1)
        pe.wait_ge(norm_step[u], i * NORM_STEPS)
        for k in range(KT):
            for m, (o, w) in enumerate(((o_hi, wo_hi), (o_hi, wo_lo), (o_lo, wo_hi))):
                for n in range(2):
                    last = nc.tensor.matmul(proj_ps[u][:, n * 512:(n + 1) * 512], o[u][:, k, :],
                                            w[:, k, n * 512:(n + 1) * 512],
                                            start=(k == 0 and m == 0), stop=(k == KT - 1 and m == 2))
        last.then_inc(proj_done[u], 1)

    def project_first(pe):
        pe.wait_ge(hand["first_norm_step"], (FT - 1) * NORM_STEPS + 1)
        project(pe, 0, 0)

    def sync(sp):
        def load_w(chunk, u, n, first=False):
            weights = at(sp, n * 2 + u)
            if not first:
                sp.wait_ge(w_ready[u], gate_tile(chunk, u, n))
            sp.dma_start(raw[u][:, 0:KT, :], w_gu[weights]).then_inc(w_in[u], 16)

        def load_d(chunk, h, j, first=False):
            weights = at(sp, j * 2 + h)
            if not first:
                sp.wait_ge(d_ready[h], chunk * KT + j)
            sp.dma_start(raw[h][:], w_d[weights]).then_inc(d_in[h], 16)

        def load_xt(dst, chunk, k, landed):
            sp.dma_start(dst.rearrange("p (n t) -> p n t", t=P),
                         x1t_dram[chunk * FT:(chunk + 1) * FT, :, k, :].rearrange("n p t -> p n t")
                         ).then_inc(landed, 16)

        def load_x_tile(i, u):
            t = at(sp, i * (2 * P) + (FCH + (2 + u) * P))
            added = at(sp, i * NORM_STEPS + 1)
            sp.wait_ge(norm_step[u], added)
            sp.dma_start(x_tok[u], x[bass.ds(t, P), :]).then_inc(x_tok_in[u], 16)

        def store_tile(i, u):
            row = at(sp, i * (2 * P) + (FCH + u * P))
            tile_no = at(sp, i * 2 + (FT + u))
            normed_at = at(sp, (i + 1) * NORM_STEPS)
            sp.wait_ge(norm_step[u], normed_at)
            sp.dma_start(x1_dram[bass.ds(row, P), :], x1[u]).then_inc(x1_stored[u], 16)
            sp.wait_ge(turned1_copied[u], i + 1)
            sp.dma_start(x1t_dram[tile_no], x1t[u]).then_inc(x1t_stored[u], 16)

        for u in range(2):
            load_x_tile(0, u)
        sp.wait_ge(hand["o_stored"], 64 * CHUNKS)
        for k in range(half_kt):
            load_xt(xt_raw[:, k, :], 0, k, xt_first_in[0])
        for u in range(2):
            load_next_o(sp, 1, u)
            store_tile(0, u)
            load_x_tile(1, u)
        for k in range(half_kt, KT):
            load_xt(xt_raw[:, k, :], 0, k, xt_first_in[1])
        for u in range(2):
            load_next_o(sp, 2, u)
            store_tile(1, u)
            load_x_tile(2, u)
        for u in range(2):
            store_tile(2, u)
        for u in range(2):
            sp.wait_ge(o_ready[u], per_u)
            load_w(0, u, 0, first=True)
        for u in range(2):
            store_tile(per_u - 1, u)

        for chunk in range(FCHUNKS):
            last = chunk == FCHUNKS - 1

            def load_pair(n):
                load_w(chunk, 0, n)
                load_w(chunk, 1, n)
            if chunk == 0:
                load_pair(1)
            loop(sp, 2, GTILES - 2, load_pair)
            load_w(chunk, 0, GTILES)
            sp.wait_ge(w_ready[0], gate_tile(chunk, 0, ICH))
            load_d(chunk, 0, 0, first=True)
            sp.wait_ge(w_ready[1], gate_tile(chunk, 1, GTILES))
            load_d(chunk, 1, 0, first=True)
            sp.wait_ge(done[0], gate_tile(chunk, 0, ICH))
            if chunk == 0:
                for u in range(2):
                    sp.wait_ge(x1_stored[u], 16 * per_u)
            for half in range(2):
                row = chunk * FCH + half * FCH // 2
                sp.dma_start(y[half], x1_dram[row:row + FCH // 2, :].rearrange("(t p) c -> p t c", p=P)
                             ).then_inc(y_in, 16)
            load_d(chunk, 0, 1)
            load_d(chunk, 1, 1)
            if not last:
                for u in range(2):
                    sp.wait_ge(x1t_stored[u], 16 * per_u)
                for k in range(half_kt):
                    load_xt(xt_raw[:, k, :], chunk + 1, k, xt_lower_in)

            def load_pieces(j):
                load_d(chunk, 0, j)
                load_d(chunk, 1, j)
            loop(sp, 2, KT - 2, load_pieces)
            if not last:
                for u in range(2):
                    sp.wait_ge(d_ready[u], (chunk + 1) * KT)
                    load_w(chunk + 1, u, 0, first=True)
                sp.wait_ge(piece_done[0], (chunk + 1) * KT)
                for k in range(half_kt, KT):
                    load_xt(xt_upper_raw[:, k - half_kt, :], chunk + 1, k, xt_upper_in)
            for half in range(2):
                for n in range(half_kt):
                    t, by_act = half * half_kt + n, n // 2
                    sp.wait_ge(normed[by_act], chunk * half_kt + 2 * half + n % 2 + 1)
                    row = chunk * FCH + t * P
                    sp.dma_start(out[row:row + P, :], y[half][:, n, :]).then_inc(y_stored[t], 16)
            if not last:
                load_w(chunk + 1, 0, 1)
                load_w(chunk + 1, 1, 1)
        for t in range(FT):
            sp.wait_ge(y_stored[t], 16 * FCHUNKS)
        for u in range(2):
            sp.wait_ge(x1_stored[u], 16 * per_u)
            sp.wait_ge(x1t_stored[u], 16 * per_u)

    def gpsimd(pool):
        def both(i):
            for u in range(2):
                pool.wait_ge(x_tok_in[u], 16 * i + 16)
                nc.gpsimd.tensor_tensor(x_tok[u], x_tok[u], bo, ALU.add).then_inc(biased[u], 1)
        loop(pool, 0, per_u, both)

    def scalar(act):
        def split_o(u, n):
            act.wait_ge(o_in[u], 16 * n + 16)
            act.wait_ge(proj_done[u], n)
            nc.scalar.copy(o_hi[u], o_raw[u]).then_inc(o_hi_ready[u], 1)

        def split_w(chunk, u, n):
            act.wait_ge(w_in[u], gate_tile(chunk, u, n) * 16 + 16)
            if isinstance(n, int) and n == 0:
                if chunk == 0:
                    act.wait_ge(proj_done[u], per_u)
                else:
                    act.wait_ge(piece_done[u], chunk * KT)
            else:
                act.wait_ge(done[u], gate_tile(chunk, u, n))
            nc.scalar.copy(slot_hi[gate_slot(chunk, u)][:, 0:KT, :], raw[u][:, 0:KT, :]).then_inc(w_hi_ready[u], 1)

        def split_d(chunk, h, j):
            act.wait_ge(d_in[h], j * 16 + (chunk * KT + 1) * 16)
            if isinstance(j, int) and j == 0:
                act.wait_ge(done[1 - h], gate_tile(chunk, 1 - h, ICH if h == 1 else GTILES))
            else:
                act.wait_ge(piece_done[h], chunk * KT + j)
            nc.scalar.copy(slot_hi[down_slot(chunk, h)][:], raw[h][:]).then_inc(d_hi_ready[h], 1)

        def split_xt(k, upper=False):
            nc.scalar.copy(row_of(xt_hi, k), xt_src(k, upper)).then_inc(xt_hi_ready, 1)

        def take_root(i, u):
            act.wait_ge(norm_step[u], i * NORM_STEPS + 5)
            nc.scalar.activation(root[:, u:u + 1], moments[:, u, 1:2], ACT.Sqrt, bias=eps[:]
                                 ).then_inc(root1_ready[u], 1)

        def take_turned(i, u):
            act.wait_ge(turned1[u], i + 1)
            act.wait_ge(x1t_stored[u], i * 16)
            nc.scalar.copy(x1t[u], turn_ps[u]).then_inc(turned1_copied[u], 1)

        def both(i, xt):
            for u in range(2):
                split_o(u, i + 1)
                take_root(i, u)
                if xt:
                    for n in range(2):
                        split_xt(i * 4 + (2 * u + n - 4))
                take_turned(i, u)
        both(0, False)
        for i in (1, 2):
            act.wait_ge(xt_first_in[i - 1], 16 * half_kt)
            both(i, True)
        take_root(per_u - 1, 0)
        split_w(0, 0, 0)
        take_turned(per_u - 1, 0)
        take_root(per_u - 1, 1)
        split_w(0, 1, 0)
        take_turned(per_u - 1, 1)
        act.wait_ge(biased[1], per_u)
        for u in range(2):
            act.wait_ge(x1t_stored[u], 16 * per_u)

        for chunk in range(FCHUNKS):
            def tile(n, rows, next_up):
                count = chunk * ICH + n
                act.wait_ge(done[0], count + 1)
                act.wait_ge(product, count)
                nc.scalar.activation(silu[0:rows, :], gate_ps[chunk][0:rows, :], ACT.Silu,
                                     scale=1.0 / 128.0).then_inc(silu_ready, 1)
                if rows < P:
                    act.wait_ge(trunc_step, count * TRUNC_STEPS)
                    nc.scalar.copy(mag[0:rows, :], gate_ps[chunk][rows:2 * rows, :]).then_inc(rest_up_ready, 1)
                else:
                    split_w(chunk, 0, n + 1)
                if next_up:
                    split_w(chunk, 1, n + 1)
                else:
                    split_d(chunk, 0 if rows == P else 1, 0)
                act.wait_ge(clipped, count + 1)
                nc.scalar.activation(mag[0:rows, :], val[0:rows, :], ACT.Abs).then_inc(mag_ready, 1)
                nc.scalar.activation(sign[0:rows, :], val[0:rows, :], ACT.Sign, scale=-1.0
                                     ).then_inc(sign_ready, 1)

            loop(act, 0, GTILES - 1, lambda n: tile(n, P, True))
            tile(GTILES - 1, P, False)
            tile(GTILES, REST, False)
            act.wait_ge(trunc_step, (chunk + 1) * ICH * TRUNC_STEPS)
            nc.scalar.copy(inner[REST:2 * REST, GTILES, :], inner[0:REST, GTILES, :].bitcast(F32)
                           ).then_inc(rest_copied, 1)

            def quantise(j, u):
                for h in range(2):
                    act.wait_ge(piece_done[h], j + (chunk * KT + 1))
                act.wait_ge(d_step, (j + chunk * WHOLE) * TRUNC_STEPS)
                nc.scalar.activation(mag[:], down_ps[chunk][u][:], ACT.Abs, scale=128.0).then_inc(d_mag_ready, 1)
                nc.scalar.activation(sign[:], down_ps[chunk][u][:], ACT.Sign).then_inc(d_sign_ready, 1)

            def quantise_half(half):
                if half == 0:
                    act.wait_ge(first_half_done, chunk + 1)
                    act.wait_ge(d_step, (chunk + 1) * WHOLE * TRUNC_STEPS)
                else:
                    act.wait_ge(piece_done[1], (chunk + 1) * KT)
                cols = slice(half * FCH // 2, (half + 1) * FCH // 2)
                nc.scalar.activation(mag[:, cols], down_ps[chunk][1][:, cols], ACT.Abs, scale=128.0
                                     ).then_inc(half_mag_ready, 1)
                nc.scalar.activation(sign[:, cols], down_ps[chunk][1][:, cols], ACT.Sign).then_inc(half_sign_ready, 1)

            def take_root(half):
                tiles = slice(half * half_kt, (half + 1) * half_kt)
                act.wait_ge(moments_ready, chunk * FT + (half + 1) * half_kt)
                nc.scalar.activation(root[:, tiles], moments[:, tiles, 1], ACT.Sqrt, bias=eps[:]
                                     ).then_inc(root_ready, 1)

            def norm(half):
                act.wait_ge(rstd_ready, 4 * chunk + 2 * half + 2)
                for n in (2, 3):
                    t = half * half_kt + n
                    nc.scalar.activation(y[half][:, n, :], y[half][:, n, :], ACT.Identity, bias=shift[:, t:t + 1],
                                         scale=rstd[:, t:t + 1]).then_inc(normed[1], 1)

            xt_piece = chunk < FCHUNKS - 1
            split_d(chunk, 0, 1)

            def pair_d(i, xt):
                for u in range(2):
                    j = i * 2 + u
                    split_d(chunk, 1, j + 1)
                    quantise(j, u)
                    split_d(chunk, 0, j + 2)
                    if xt:
                        split_xt(j)
            if xt_piece:
                act.wait_ge(xt_lower_in, 16 * half_kt)
                loop(act, 0, half_kt // 2, lambda i: pair_d(i, True))
                pair_d(half_kt // 2, False)
            else:
                loop(act, 0, KT // 2 - 1, lambda i: pair_d(i, False))
            split_d(chunk, 1, KT - 1)
            quantise(KT - 2, 0)
            quantise_half(0)
            if xt_piece:
                split_w(chunk + 1, 0, 0)
            take_root(0)
            quantise_half(1)
            if xt_piece:
                split_w(chunk + 1, 1, 0)
            norm(0)
            take_root(1)
            norm(1)
            if xt_piece:
                act.wait_ge(xt_upper_in, 16 * half_kt)
                for n in range(half_kt):
                    act.wait_ge(y_stored[n], 16)
                    split_xt(half_kt + n, upper=True)

    def vector(dve):
        def low(dst, src, hi):
            return nc.vector.tensor_tensor(dst, src, hi.bitcast(F32), ALU.subtract)

        def split_o(u, n):
            dve.wait_ge(o_hi_ready[u], n + 1)
            low(o_lo[u], o_raw[u], o_hi[u]).then_inc(o_ready[u], 1)

        def split_w(chunk, u, n):
            s = gate_slot(chunk, u)
            dve.wait_ge(w_hi_ready[u], gate_tile(chunk, u, n) + 1)
            low(slot_lo[s][:, 0:KT, :], raw[u][:, 0:KT, :], slot_hi[s][:, 0:KT, :]).then_inc(w_ready[u], 1)

        def split_d(chunk, h, j):
            s = down_slot(chunk, h)
            dve.wait_ge(d_hi_ready[h], j + (chunk * KT + 1))
            if h == 0:
                low(slot_lo[s][:], raw[h][:], slot_hi[s][:]).then_inc(d_ready[h], 1)
            else:
                rest = slice(REST, 2 * REST)
                low(slot_lo[s][:, 0:PIECE - 1, :], raw[h][:, 0:PIECE - 1, :], slot_hi[s][:, 0:PIECE - 1, :]
                    ).then_inc(d_rest, 1)
                low(slot_hi[s][rest, PIECE - 1, :], raw[h][rest, PIECE - 1, :], slot_hi[s][rest, PIECE - 1, :]
                    ).then_inc(d_ready[h], 1)

        def split_xt(k, upper=False):
            low(row_of(xt_lo, k), xt_src(k, upper), row_of(xt_hi, k)).then_inc(xt_ready, 1)

        def take_xt(k):
            dve.wait_ge(xt_hi_ready, k + 1)
            split_xt(k)

        split_lo(dve, 1)

        def tile(i, u, split):
            step = i * NORM_STEPS
            dve.wait_ge(proj_done[u], i + 1)
            dve.wait_ge(biased[u], i + 1)
            nc.vector.tensor_tensor(y_tok[u], proj_ps[u][:], x_tok[u], ALU.add).then_inc(norm_step[u], 1)
            dve.wait_ge(norm_step[u], step + 1)
            for n in range(2):
                nc.vector.bn_stats(stats[:, u, n, :], y_tok[u][:, n * 512:(n + 1) * 512]).then_inc(norm_step[u], 1)
            if split:
                split_o(u, i + 1)
            dve.wait_ge(norm_step[u], step + 3)
            nc.vector.bn_aggr(moments[:, u, :], stats[:, u, 0:2, :]).then_inc(norm_step[u], 2)
            dve.wait_ge(root1_ready[u], i + 1)
            nc.vector.reciprocal(rstd[:, u:u + 1], root[:, u:u + 1]).then_inc(norm_step[u], 1)
            dve.wait_ge(norm_step[u], step + 6)
            dve.wait_ge(x1_stored[u], 16 * i)
            dve.wait_ge(turned1[u], i)
            nc.vector.tensor_scalar(x1[u], y_tok[u], moments[:, u, 0:1], rstd[:, u:u + 1],
                                    ALU.subtract, ALU.mult).then_inc(norm_step[u], 1)

        def both(i, xt):
            for u in range(2):
                tile(i, u, True)
                if xt:
                    for n in range(2):
                        take_xt(i * 4 + (2 * u + n - 4))
        for u in range(2):
            dve.wait_ge(hand["first_x1_stored"][u], 16 * per_u)
            dve.wait_ge(hand["x1_turned"], FT - 1 + u)
            tile(0, u, True)
        loop(dve, 1, 2, lambda i: both(i, True))
        tile(per_u - 1, 0, False)
        split_w(0, 0, 0)
        tile(per_u - 1, 1, False)
        split_w(0, 1, 0)
        for u in range(2):
            dve.wait_ge(x1t_stored[u], 16 * per_u)
            dve.wait_ge(x1_stored[u], 16 * per_u)

        for chunk in range(FCHUNKS):
            def tile_g(n, rows, next_up):
                r = slice(0, rows)
                count = chunk * ICH + n
                step = count * TRUNC_STEPS
                if rows == P:
                    split_w(chunk, 0, n + 1)
                dve.wait_ge(silu_ready, count + 1)
                dve.wait_ge(sign_ready, count)
                if rows == P:
                    dve.wait_ge(done[1], gate_tile(chunk, 1, n) + 1)
                    nc.vector.tensor_tensor(val[r, :], up_ps[r, :], silu[r, :], ALU.mult).then_inc(product, 1)
                else:
                    dve.wait_ge(rest_up_ready, chunk + 1)
                    nc.vector.tensor_tensor(val[r, :], mag[r, :], silu[r, :], ALU.mult).then_inc(product, 1)
                dve.wait_ge(product, count + 1)
                nc.vector.tensor_scalar(val[r, :], val[r, :], -128.0, 127.0, ALU.max, ALU.min).then_inc(clipped, 1)
                if next_up:
                    split_w(chunk, 1, n + 1)
                else:
                    split_d(chunk, 0 if rows == P else 1, 0)
                dve.wait_ge(mag_ready, count + 1)
                nc.vector.tensor_scalar(near[r, :], mag[r, :], ROUND, ROUND, ALU.add, ALU.subtract
                                        ).then_inc(trunc_step, 1)
                dve.wait_ge(trunc_step, step + 1)
                nc.vector.tensor_tensor(mag[r, :], near[r, :], mag[r, :], ALU.is_gt).then_inc(trunc_step, 1)
                dve.wait_ge(trunc_step, step + 2)
                nc.vector.tensor_tensor(near[r, :], mag[r, :], near[r, :], ALU.subtract).then_inc(trunc_step, 1)
                dve.wait_ge(trunc_step, step + 3)
                dve.wait_ge(sign_ready, count + 1)
                nc.vector.tensor_tensor(inner[r, bass.ds(n, 1), :].rearrange("p a t -> p (a t)"), near[r, :],
                                        sign[r, :], ALU.mult).then_inc(trunc_step, 2)

            loop(dve, 0, GTILES - 1, lambda n: tile_g(n, P, True))
            tile_g(GTILES - 1, P, False)
            tile_g(GTILES, REST, False)

            def truncate_columns(cols, mag_at, sign_at, counts, at_step):
                mag_sem, sign_sem, step_sem = counts
                dve.wait_ge(mag_sem, mag_at)
                nc.vector.tensor_scalar(val[:, cols], mag[:, cols], 128.0, ROUND, ALU.min, ALU.add
                                        ).then_inc(step_sem, 1)
                dve.wait_ge(step_sem, at_step + 1)
                nc.vector.scalar_tensor_tensor(mag[:, cols], val[:, cols], ROUND, mag[:, cols], ALU.subtract,
                                               ALU.is_gt).then_inc(step_sem, 1)
                dve.wait_ge(step_sem, at_step + 2)
                nc.vector.scalar_tensor_tensor(near[:, cols], val[:, cols], ROUND, mag[:, cols], ALU.subtract,
                                               ALU.subtract).then_inc(step_sem, 1)
                dve.wait_ge(step_sem, at_step + 3)
                dve.wait_ge(sign_sem, sign_at)
                nc.vector.tensor_tensor(near[:, cols], near[:, cols], sign[:, cols], ALU.mult).then_inc(step_sem, 2)

            def truncate(j):
                count = j + chunk * WHOLE
                dve.wait_ge(turned, count)
                truncate_columns(slice(0, FCH), count + 1, count + 1, (d_mag_ready, d_sign_ready, d_step),
                                 count * TRUNC_STEPS)

            def truncate_half(half):
                dve.wait_ge(turned, (chunk + 1) * WHOLE)
                count = 2 * chunk + half
                truncate_columns(slice(half * FCH // 2, (half + 1) * FCH // 2), count + 1, count + 1,
                                 (half_mag_ready, half_sign_ready, half_step), count * TRUNC_STEPS)

            def add_to(half, j):
                c = bass.ds(j * P, P)
                tiles = slice(half * half_kt, (half + 1) * half_kt)
                return nc.vector.scalar_tensor_tensor(y[half][:, :, c], quant_ps[chunk][:, tiles, :], 127.0,
                                                      y[half][:, :, c], ALU.min, ALU.add)

            def count_to(half, j):
                for n in range(half_kt):
                    last = nc.vector.bn_stats(stats[:, half * half_kt + n, bass.ds(j, 1), :].rearrange(
                        "p a s -> p (a s)"), y[half][:, n, bass.ds(j * P, P)])
                return last

            def add(j):
                dve.wait_ge(turned, j + (chunk * WHOLE + 1))
                for half in range(2):
                    add_to(half, j).then_inc(added, 1)

            def count_in(j):
                dve.wait_ge(added, (j + chunk * WHOLE) * 2 + 2)
                for half in range(2):
                    last = count_to(half, j)
                last.then_inc(counted, 1)

            def finish_half(half):
                count = 2 * chunk + half
                dve.wait_ge(half_turned, count + 1)
                add_to(half, KT - 1).then_inc(half_added, 1)
                dve.wait_ge(half_added, count + 1)
                count_to(half, KT - 1).then_inc(half_counted, 1)
                dve.wait_ge(counted, (chunk + 1) * WHOLE)
                dve.wait_ge(half_counted, count + 1)
                tiles = slice(half * half_kt, (half + 1) * half_kt)
                for t in range(half * half_kt, (half + 1) * half_kt):
                    nc.vector.bn_aggr(moments[:, t, :], stats[:, t, :, :]).then_inc(moments_ready, 1)
                dve.wait_ge(root_ready, count + 1)
                nc.vector.reciprocal(rstd[:, tiles], root[:, tiles]).then_inc(rstd_ready, 1)
                dve.wait_ge(rstd_ready, 2 * count + 1)
                nc.vector.scalar_tensor_tensor(shift[:, tiles], moments[:, tiles, 0], -1.0, rstd[:, tiles],
                                               ALU.mult, ALU.mult).then_inc(rstd_ready, 1)
                for n in (0, 1):
                    t = half * half_kt + n
                    nc.vector.tensor_scalar(y[half][:, n, :], y[half][:, n, :], moments[:, t, 0:1], rstd[:, t:t + 1],
                                            ALU.subtract, ALU.mult).then_inc(normed[0], 1)

            xt_piece = chunk < FCHUNKS - 1

            def take_next_xt(k, upper=False):
                dve.wait_ge(xt_hi_ready, k + (KT + 1))
                split_xt(k, upper)

            split_d(chunk, 0, 1)
            split_d(chunk, 1, 1)
            truncate(0)
            split_d(chunk, 0, 2)
            dve.wait_ge(y_in, 32 * (chunk + 1))

            def step_d(j, xt=False):
                if xt:
                    take_next_xt(j - 2)
                split_d(chunk, 1, j)
                add(j - 2)
                count_in(j - 2)
                truncate(j - 1)
                split_d(chunk, 0, j + 1)
            if xt_piece:
                loop(dve, 2, half_kt, lambda j: step_d(j, xt=True))
                step_d(KT - 2)
            else:
                loop(dve, 2, KT - 3, step_d)
            split_d(chunk, 1, KT - 1)
            add(KT - 3)
            count_in(KT - 3)
            truncate(KT - 2)
            truncate_half(0)
            add(KT - 2)
            count_in(KT - 2)
            if xt_piece:
                split_w(chunk + 1, 0, 0)
            finish_half(0)
            truncate_half(1)
            if xt_piece:
                split_w(chunk + 1, 1, 0)
            finish_half(1)
            if xt_piece:
                for k in range(half_kt, KT):
                    dve.wait_ge(y_stored[k], 16)
                    take_next_xt(k, upper=True)

    def tensor(pe):
        def turn_x1(i, u):
            pe.wait_ge(norm_step[u], (i + 1) * NORM_STEPS)
            pe.wait_ge(turned1_copied[u], i)
            for k in range(KT):
                last = nc.tensor.transpose(turn_ps[u][:, k, :], x1[u][:, k * P:(k + 1) * P], ident[:])
            last.then_inc(turned1[u], 1)

        def both(i):
            project(pe, i, 1)
            if isinstance(i, int) and i == 0:
                pe.wait_ge(hand["o_copied"], ATT_BATCHES)
            turn_x1(i, 0)
            project(pe, i + 1, 0)
            turn_x1(i, 1)
        pe.wait_ge(hand["x1t_copied"], FT)
        loop(pe, 0, per_u - 1, both)
        project(pe, per_u - 1, 1)
        turn_x1(per_u - 1, 0)

        def products(chunk, u, ks):
            s = gate_slot(chunk, u)
            ps = up_ps if u else gate_ps[chunk]
            for k in ks:
                for m, (w, xt) in enumerate(((slot_hi, xt_hi), (slot_hi, xt_lo), (slot_lo, xt_hi))):
                    for h in range(2):
                        last = nc.tensor.matmul(ps[:, h * 512:(h + 1) * 512], w[s][:, k, :],
                                                xt[:, k, h * 512:(h + 1) * 512],
                                                start=(k == 0 and m == 0), stop=(k == KT - 1 and m == 2))
            return last

        def tile_g(chunk, u, n):
            pe.wait_ge(w_ready[u], gate_tile(chunk, u, n) + 1)
            pe.wait_ge(product if u else silu_ready, chunk * ICH + n)
            products(chunk, u, range(KT)).then_inc(done[u], 1)

        def piece(chunk, j, u, h, first=False):
            s = down_slot(chunk, h)
            pe.wait_ge(d_ready[h], j + (chunk * KT + 1))
            for c in range(PIECE):
                rest = h == 1 and c == PIECE - 1
                if rest and first:
                    pe.wait_ge(rest_copied, chunk + 1)
                for m, w in enumerate((slot_hi,) if rest else (slot_hi, slot_lo)):
                    for half in range(2):
                        last = nc.tensor.matmul(down_ps[chunk][u][:, half * 512:(half + 1) * 512], w[s][:, c, :],
                                                inner[:, h * PIECE + c, half * 512:(half + 1) * 512],
                                                start=(h == 0 and c == 0 and m == 0), stop=rest)
            last.then_inc(piece_done[h], 1)

        def half_piece(chunk, h, half):
            s = down_slot(chunk, h)
            pe.wait_ge(d_ready[h], (chunk + 1) * KT)
            cols = slice(half * 512, (half + 1) * 512)
            for c in range(PIECE):
                rest = h == 1 and c == PIECE - 1
                for m, w in enumerate((slot_hi,) if rest else (slot_hi, slot_lo)):
                    last = nc.tensor.matmul(down_ps[chunk][1][:, cols], w[s][:, c, :], inner[:, h * PIECE + c, cols],
                                            start=(h == 0 and c == 0 and m == 0), stop=rest)
            return last

        def turn_half(chunk, half):
            pe.wait_ge(half_step, (2 * chunk + half + 1) * TRUNC_STEPS)
            pe.wait_ge(added, (chunk + 1) * WHOLE * 2)
            for t in range(half * half_kt, (half + 1) * half_kt):
                last = nc.tensor.transpose(quant_ps[chunk][:, t, :], near[:, t * P:(t + 1) * P], ident_bf[:])
            last.then_inc(half_turned, 1)

        def turn_quant(chunk, j):
            count = j + chunk * WHOLE
            pe.wait_ge(d_step, count * TRUNC_STEPS + TRUNC_STEPS)
            pe.wait_ge(added, count * 2)
            for t in range(FT):
                last = nc.tensor.transpose(quant_ps[chunk][:, t, :], near[:, t * P:(t + 1) * P], ident_bf[:])
            last.then_inc(turned, 1)

        for u in range(2):
            pe.wait_ge(xt_ready, KT)
            pe.wait_ge(norm_step[u], (per_u - 1) * NORM_STEPS + 1)
            if u == 0:
                tile_g(0, 0, 0)
                turn_x1(per_u - 1, 1)
            else:
                tile_g(0, 1, 0)

        for chunk in range(FCHUNKS):
            last_chunk = chunk == FCHUNKS - 1

            def pair_g(n):
                tile_g(chunk, 0, n)
                tile_g(chunk, 1, n)
            loop(pe, 1, GTILES - 1, pair_g)
            pe.wait_ge(silu_ready, chunk * ICH + GTILES)
            tile_g(chunk, 0, GTILES)

            pe.wait_ge(half_added, 2 * chunk)
            pe.wait_ge(trunc_step, (chunk * ICH + PIECE) * TRUNC_STEPS)
            piece(chunk, 0, 0, 0)
            pe.wait_ge(trunc_step, (chunk * ICH + GTILES) * TRUNC_STEPS)
            piece(chunk, 0, 0, 1, first=True)
            pe.wait_ge(half_sign_ready, 2 * chunk)
            piece(chunk, 1, 1, 0)
            piece(chunk, 1, 1, 1)
            turn_quant(chunk, 0)

            def output_tile(j, u):
                pe.wait_ge(d_sign_ready, j - 1 + chunk * WHOLE)
                piece(chunk, j, u, 0)
                piece(chunk, j, u, 1)
                turn_quant(chunk, j - 1)

            def pair_d(i):
                for u in range(2):
                    output_tile(i * 2 + u, u)
            loop(pe, 1, KT // 2 - 2, pair_d)
            output_tile(KT - 2, 0)
            pe.wait_ge(d_sign_ready, (chunk + 1) * WHOLE - 1)
            half_piece(chunk, 0, 0)
            half_piece(chunk, 1, 0).then_inc(first_half_done, 1)
            turn_quant(chunk, KT - 2)
            half_piece(chunk, 0, 1).then_inc(piece_done[0], 1)
            turn_half(chunk, 0)
            half_piece(chunk, 1, 1).then_inc(piece_done[1], 1)
            if not last_chunk:
                nxt = chunk + 1
                pe.wait_ge(xt_ready, KT + half_kt)
                pe.wait_ge(d_sign_ready, (chunk + 1) * WHOLE)
                pe.wait_ge(w_ready[0], gate_tile(nxt, 0, 0) + 1)
                products(nxt, 0, (0, 1))
            turn_half(chunk, 1)
            if not last_chunk:
                products(nxt, 0, (2, 3))
                pe.wait_ge(w_ready[1], gate_tile(nxt, 1, 0) + 1)
                products(nxt, 1, (0,))
            if not last_chunk:
                products(nxt, 1, range(1, half_kt))
                for u, k in ((0, 4), (1, 4), (0, 5), (1, 5), (0, 6), (0, 7), (1, 6), (1, 7)):
                    pe.wait_ge(xt_ready, KT + k + 1)
                    last = products(nxt, u, (k,))
                    if k == KT - 1:
                        last.then_inc(done[u], 1)

    return ({"sync": sync, "gpsimd": gpsimd, "scalar": scalar, "vector": vector, "tensor": tensor},
            {"load_o": load_o, "load_next_o": load_next_o, "load_x": load_x,
              "split_hi": split_hi, "split_lo": split_lo, "project": project_first})


def build(nc, ins, out):
    qkv_dram = nc.dram_tensor("qkv_scratch", (CHUNKS, 8, 3 * HID, HALF), F32).ap()
    o_dram = nc.dram_tensor("o_scratch", (HID, TOKENS), F32).ap()
    x1_dram = nc.dram_tensor("x1_scratch", (TOKENS, HID), F32).ap()
    x1t_dram = nc.dram_tensor("x1t_scratch", (OUT_TILES, P, KT, P), F32).ap()
    with ExitStack() as ctx:
        m = memory(nc, ctx)

        def sem(name):
            return ctx.enter_context(nc.semaphore(name))
        hand = {n: sem(n) for n in ("q_packed", "k_placed", "v_copied", "o_copied", "o_stored", "first_norm_step",
                                    "x1_turned", "x1t_copied")}
        for n in ("first_x1_stored", "first_x1t_stored"):
            hand[n] = [sem(f"{n}{u}") for u in range(2)]
        later, start = later_programs(nc, ctx, m, hand, o_dram, ins["x"], ins["w_gu"], ins["w_d"], x1_dram, x1t_dram,
                                      out)
        first = attention_programs(nc, ctx, m, hand, start, ins["x_t"], ins["w_qkv"], ins["b_qkv"], ins["identity"],
                                   ins["identity_bf"], qkv_dram, o_dram, ins["w_o"], ins["b_o"], ins["x"], x1_dram,
                                   x1t_dram)
        block = ctx.enter_context(nc.Block())

        @block.sync
        def _(sp):
            first["sync"](sp)
            later["sync"](sp)

        @block.gpsimd
        def _(pool):
            first["gpsimd"](pool)
            later["gpsimd"](pool)

        @block.scalar
        def _(act):
            first["scalar"](act)
            later["scalar"](act)

        @block.vector
        def _(dve):
            first["vector"](dve)
            later["vector"](dve)

        @block.tensor
        def _(pe):
            first["tensor"](pe)
            later["tensor"](pe)


def kernel(L0_attn_x, L0_attn_Wq, L0_attn_bq, L0_attn_Wk, L0_attn_bk, L0_attn_Wv, L0_attn_bv, L0_attn_Wo,
           L0_attn_bo, L0_ffn_w_gate, L0_ffn_w_up, L0_ffn_w_down):
    import ml_dtypes
    import concourse.bacc as bacc
    from concourse.bass_utils import run_bass_kernel_spmd

    shape = L0_attn_x.shape
    x = np.ascontiguousarray(L0_attn_x).reshape(TOKENS, HID)

    def tiles(w):
        return np.asarray(w).reshape(-1, P, KT, P).transpose(0, 3, 2, 1)

    def by_channel(w):
        w = np.asarray(w)
        return w.reshape(HEADS, HD, -1).swapaxes(0, 1).reshape(w.shape)

    gate, up = np.asarray(L0_ffn_w_gate), np.asarray(L0_ffn_w_up)
    whole = GTILES * P
    pairs = np.stack([tiles(gate[:whole]), tiles(up[:whole])], axis=1).reshape(2 * GTILES, P, KT, P)
    rest = tiles(np.concatenate([gate[whole:], up[whole:]]))
    wd = np.asarray(L0_ffn_w_down)
    wd = np.concatenate([wd, wd[:, whole:]], axis=1).reshape(KT, P, 2, PIECE, P).transpose(0, 2, 4, 3, 1)
    wd = wd.reshape(2 * KT, P, PIECE, P)
    arrays = {
        "x": x,
        "x_t": x.reshape(CHUNKS, CHUNK, KT, P).transpose(0, 3, 2, 1),
        "w_qkv": tiles(np.concatenate([by_channel(w) for w in (L0_attn_Wq, L0_attn_Wk, L0_attn_Wv)])),
        "b_qkv": np.concatenate([by_channel(b) for b in (L0_attn_bq, L0_attn_bk, L0_attn_bv)]
                                ).reshape(QKV_TILES, P).T,
        "w_o": np.asarray(L0_attn_Wo).T.reshape(KT, P, HID),
        "b_o": np.asarray(L0_attn_bo),
        "identity": np.eye(P, dtype=np.float32),
        "identity_bf": np.eye(P, dtype=ml_dtypes.bfloat16),
        "w_gu": np.concatenate([pairs, rest]),
        "w_d": wd,
    }
    nc = bacc.Bacc("TRN2", target_bir_lowering=False, num_devices=1)
    arrays = {n: np.ascontiguousarray(a) for n, a in arrays.items()}
    ins = {n: nc.dram_tensor(f"in_{n}", a.shape, mybir.dt.from_np(a.dtype), kind="ExternalInput").ap()
           for n, a in arrays.items()}
    out = nc.dram_tensor("out", (TOKENS, HID), F32, kind="ExternalOutput").ap()
    build(nc, ins, out)
    run = run_bass_kernel_spmd(nc, [{f"in_{n}": a for n, a in arrays.items()}], core_ids=[0])
    return run.results[0]["out"].reshape(shape)
```
